# Optimizing a Trainium2 kernel written in Bass

```python
import numpy as np
import jax
import jax.numpy as jnp

def _softmax(x, axis=-1):
    return jax.nn.softmax(x, axis=axis)

def _gelu(x):
    return jax.nn.gelu(x, approximate=True)

def _silu(x):
    return jax.nn.silu(x)

def _sigmoid(x):
    return jax.nn.sigmoid(x)

def _layernorm(x, axis=-1, eps=1e-05):
    m = jnp.mean(x, axis=axis, keepdims=True)
    v = jnp.var(x, axis=axis, keepdims=True)
    return (x - m) / jnp.sqrt(v + eps)

def _scatter_add(tgt, idx, src, axis=0):
    return tgt.at[idx].add(src)

def _segment_sum(src, seg, n):
    return jax.ops.segment_sum(src, seg, n)
kernel_name = 'mk_gnn_ffn_d1_gnn_r8_42f988'

def setup_inputs(seed: int=0):
    np.random.seed(seed)
    _w = jnp.asarray

    def _rec_inputs():
        import jax
        import jax.numpy as jnp
        _gk = jax.random.key(seed)
        x = -0.0006008 + 1.001 * jax.random.normal(jax.random.fold_in(_gk, 1), (6250, 256), jnp.float32)
        src = jax.random.randint(jax.random.fold_in(_gk, 2), (100000,), 0, 6250, jnp.int32)
        dst = jax.random.randint(jax.random.fold_in(_gk, 3), (100000,), 0, 6250, jnp.int32)
        _o = jnp.argsort(dst, stable=True)
        src = src[_o]
        dst = dst[_o]
        return (x, src, dst)
    x, src, dst = _rec_inputs()

    def _L0_gnn_setup():
        import jax, jax.numpy as jnp
        import numpy as np
        N_NODES = 1250
        key = jax.random.key(seed)
        k1, k2, k3, k4 = jax.random.split(key, 4)
        h = jax.random.normal(k1, (N_NODES, 256), dtype=jnp.float32)
        edge_index = jax.random.randint(k2, (2, 40000), 0, N_NODES, dtype=jnp.int64)
        W = jax.random.normal(k3, (256, 512), dtype=jnp.float32) * (1.0 / np.sqrt(512.0))
        b = jax.random.normal(k4, (256,), dtype=jnp.float32) * 0.01
        return {'h': h, 'edge_index': edge_index, 'W': W, 'b': b}
    _L0_gnn_all = _L0_gnn_setup()
    _L0_gnn_in = {k: v for k, v in _L0_gnn_all.items() if k in ('W', 'b')}
    del _L0_gnn_all

    def _L0_ffn_setup():
        import jax, jax.numpy as jnp
        import numpy as np
        E = 8
        K = 2
        D = 256
        H = 512
        DOUT = 256
        EPS = 1e-05
        key = jax.random.key(seed)
        ks = jax.random.split(key, 9)
        s = 0.02
        return {'x': jax.random.normal(ks[0], (4, 1024, D), jnp.float32), 'gamma': 1.0 + 0.05 * jax.random.normal(ks[1], (D,), jnp.float32), 'beta': 0.05 * jax.random.normal(ks[2], (D,), jnp.float32), 'Wr': 0.01 * jax.random.normal(ks[3], (D, E), jnp.float32), 'br': jnp.zeros((E,), jnp.float32), 'W1': s * jax.random.normal(ks[4], (E, D, H), jnp.float32), 'b1': s * jax.random.normal(ks[5], (E, H), jnp.float32), 'W2': s * jax.random.normal(ks[6], (E, H, DOUT), jnp.float32), 'b2': s * jax.random.normal(ks[7], (E, DOUT), jnp.float32)}
    _L0_ffn_all = _L0_ffn_setup()
    _L0_ffn_in = {k: v for k, v in _L0_ffn_all.items() if k in ('gamma', 'beta', 'Wr', 'br', 'W1', 'b1', 'W2', 'b2')}
    del _L0_ffn_all
    return {'x': x, 'src': src, 'dst': dst, 'L0_gnn_W': _L0_gnn_in['W'], 'L0_gnn_b': _L0_gnn_in['b'], 'L0_ffn_gamma': _L0_ffn_in['gamma'], 'L0_ffn_beta': _L0_ffn_in['beta'], 'L0_ffn_Wr': _L0_ffn_in['Wr'], 'L0_ffn_br': _L0_ffn_in['br'], 'L0_ffn_W1': _L0_ffn_in['W1'], 'L0_ffn_b1': _L0_ffn_in['b1'], 'L0_ffn_W2': _L0_ffn_in['W2'], 'L0_ffn_b2': _L0_ffn_in['b2']}

def reference(x, src, dst, L0_gnn_W, L0_gnn_b, L0_ffn_gamma, L0_ffn_beta, L0_ffn_Wr, L0_ffn_br, L0_ffn_W1, L0_ffn_b1, L0_ffn_W2, L0_ffn_b2):
    import jax
    import jax.numpy as jnp

    def _L0_gnn_ref(h, edge_index, W, b):
        import jax, jax.numpy as jnp
        import numpy as np
        N_NODES = 1250
        src, dst = (edge_index[0], edge_index[1])
        n = h.shape[0]
        msg_sum = jax.ops.segment_sum(h[src], dst, num_segments=n)
        deg = jax.ops.segment_sum(jnp.ones_like(src, dtype=h.dtype), dst, num_segments=n)
        agg = msg_sum / jnp.maximum(deg, 1.0)[:, None]
        h_total = jnp.concatenate([h, agg], axis=1)
        return h_total @ W.T + b

    def _L0_ffn_ref(x, gamma, beta, Wr, br, W1, b1, W2, b2):
        import jax, jax.numpy as jnp
        import numpy as np
        E = 8
        K = 2
        D = 256
        H = 512
        DOUT = 256
        EPS = 1e-05
        mu = jnp.mean(x, axis=-1, keepdims=True)
        var = jnp.mean(jnp.square(x - mu), axis=-1, keepdims=True)
        xn = (x - mu) * jax.lax.rsqrt(var + EPS) * gamma + beta
        logits = jnp.einsum('bsd,de->bse', xn, Wr) + br
        top_vals, top_idx = jax.lax.top_k(logits, K)
        w = jax.nn.softmax(top_vals, axis=-1)
        w_full = jnp.einsum('bsk,bske->bse', w, jax.nn.one_hot(top_idx, E, dtype=w.dtype))
        y = jnp.zeros(x.shape[:-1] + (DOUT,), x.dtype)
        for e in range(E):
            h = jax.nn.gelu(jnp.einsum('bsd,dh->bsh', xn, W1[e]) + b1[e], approximate=False)
            y_e = jnp.einsum('bsh,hd->bsd', h, W2[e]) + b2[e]
            y = y + y_e * w_full[..., e, None]
        return y
    edge_index = jnp.stack([src, dst])
    x = x + _L0_gnn_ref(_layernorm(x, axis=-1), edge_index, L0_gnn_W, L0_gnn_b)
    x = x + _L0_ffn_ref(_layernorm(x, axis=-1)[None], L0_ffn_gamma, L0_ffn_beta, L0_ffn_Wr, L0_ffn_br, L0_ffn_W1, L0_ffn_b1, L0_ffn_W2, L0_ffn_b2)[0]
    return x

_drawn_inputs = setup_inputs


def setup_inputs(seed=0):
    import zlib

    import numpy as np

    out = dict(_drawn_inputs(seed))
    spreads = {'L0_ffn_br': (0.0, 0.1)}
    factors = {'L0_gnn_b': 7.441,
     'L0_ffn_gamma': 7.443,
     'L0_ffn_beta': 6.444,
     'L0_ffn_b1': 8.0,
     'L0_ffn_b2': 5.237}
    for name, (base, spread) in spreads.items():
        noise = np.random.default_rng([zlib.crc32(name.encode()), seed]).standard_normal(out[name].shape)
        drawn = base * np.exp(spread * noise) if base else spread * noise
        out[name] = jnp.asarray(drawn.astype(out[name].dtype))
    for name, factor in factors.items():
        out[name] = (out[name] * factor).astype(out[name].dtype)
    return out
```

```python
from contextlib import ExitStack

import concourse.bass as bass
from concourse import mybir

F32 = mybir.dt.float32
BF16 = mybir.dt.bfloat16
I32 = mybir.dt.int32
U32 = mybir.dt.uint32
ALU = mybir.AluOpType
ACT = mybir.ActivationFunctionType
AX_X = mybir.AxisListType.X
ds = bass.ds

P = 128
EPS = 1e-5


class Event:

    def __init__(self, nc, name, per=1, credit_by=None):
        self.sem = nc.alloc_semaphore(name)
        self.per, self.done, self.credit = per, 0, 0
        if credit_by is not None:
            self.credit = per
            credit_by.sem_inc(self.sem, per)

    def inc(self, instruction):
        instruction.then_inc(self.sem, 1)
        self.done += 1
        return self.done

    def wait(self, engine, n=None, round=0, back=0, apart=False):
        n = self.per if n is None else n
        value = round * self.per + (n + self.credit - back * self.per)
        if apart and not isinstance(round, int):
            value = engine.to_reg(value)
            engine.wait_ge(self.sem, 1)
        engine.wait_ge(self.sem, value)


class Chain(Event):

    def begin(self, round=0):
        self.done, self.round = 0, round

    def then(self, engine, instruction, apart=False):
        n = self.inc(instruction)
        self.wait(engine, n, self.round, apart=apart)
        return n

    def end(self):
        assert self.done == self.per, (self.done, self.per)


def build(nc, x, src, dst, gnn_w, gnn_b, gamma, beta, wr, br, w1, b1, w2, b2, out):
    pe, dve, act, pool, sp = nc.tensor, nc.vector, nc.scalar, nc.gpsimd, nc.sync
    N, D = x.shape
    (E,) = src.shape
    X, _, H = w1.shape
    DO = w2.shape[2]
    DC = D // P
    HC = H // P
    NT = -(-N // P)
    ET = -(-E // P)
    TAIL = N - (NT - 1) * P
    B = 7
    NB = NT // B
    assert NT == B * NB and NB % 2 == 1 and D == 256 and DO == D and H == 512 and X == 8
    SPR = 17
    STEPS = SPR * NT
    assert STEPS >= ET + NT - 1
    HALF = 9
    SB = STEPS // B
    assert SB * B == STEPS and SB <= P
    TABLE = STEPS - NT + 1
    FIRSTS = ET - 1
    ROW = D + 4
    QUEUE = (NT + 1) * P
    IDLE = X * QUEUE
    TRASH = IDLE + P
    QROWS = TRASH + 2 * P
    QUEUE_TILES = (2 * N + X * (P - 1)) // P
    PAIRS = -(-QUEUE_TILES // 2)
    QT = 2 * PAIRS + 4
    OUT_ROWS = out.shape[0]
    assert OUT_ROWS >= N + P and OUT_ROWS >= NT * P

    def sb(name, shape, dt=F32):
        return nc.alloc_sbuf_tensor(name, shape, dt)

    h_rows = nc.dram_tensor("h_rows", (NT * P, D), F32).ap()
    src_tab = nc.dram_tensor("src_tab", (TABLE * P,), I32).ap()
    dst_tab = nc.dram_tensor("dst_tab", (TABLE * P,), I32).ap()
    b1_new = nc.dram_tensor("b1_new", (X, H), F32).ap()
    queue = nc.dram_tensor("queue", (QROWS, ROW), F32).ap()

    w1_sb = sb("w1_sb", [P, X, DC, H])
    region = sb("region", [P, X * HC * DO])
    xall = sb("xall", [P, NT, D])
    GW = D + 1
    acc = sb("acc", [P, NT * GW])
    acc3 = acc[:, :].rearrange("p (t c) -> p t c", t=NT)
    pay = sb("pay", [P, 2, B, ROW])
    pairbuf = sb("pairbuf", [P, 4, D])
    rowsb, trsb = pairbuf[:, 0:2, :], pairbuf[:, 2:4, :]
    wgt = sb("wgt", [P, 2 * DC, D])
    ident = sb("ident", [P, P])
    ones = sb("ones", [P, P])
    tri_b = sb("tri_b", [P, P], BF16)
    ones_b = sb("ones_b", [P, P], BF16)
    iota = sb("iota", [P, P])
    pcol = sb("pcol", [P, 1])
    pcol_i = sb("pcol_i", [P, 1], I32)
    gb_row = sb("gb_row", [1, D])
    n_row = sb("n_row", [1, STEPS], I32)
    mv = sb("mv", [P, B, 2])
    rstd = sb("rstd", [P, NT])
    nmr = sb("nmr", [P, NT])
    stats = sb("stats", [P, B, 6])
    sd = sb("sd", [P, B])
    idx_a = sb("idx_a", [P, HALF], I32)
    idx_b = sb("idx_b", [P, SPR - HALF], I32)
    wr_sb = sb("wr_sb", [P, DC, X])
    br_row = sb("br_row", [1, X])
    gam = sb("gam", [P, DC])
    bet = sb("bet", [P, DC])

    def at(base, offset, *shape):
        n = 1
        for s in shape:
            n *= s
        v = base[:, offset:offset + n]
        if len(shape) == 2:
            v = v.rearrange("p (a b) -> p a b", a=shape[0])
        return v, offset + n

    pay_flat = pay[:, :, :, :].rearrange("p a b c -> p (a b c)")
    fst_i, o = at(region, 0, FIRSTS)
    fst_f, o = at(region, o, FIRSTS)
    below, o = at(region, o, FIRSTS)
    passed, o = at(region, o, STEPS)
    tab_i, o = at(region, o, 2 * B, P)
    tab_f, o = at(region, o, 2 * B, P)
    fst_i, tab_i = fst_i.bitcast(I32), tab_i.bitcast(I32)
    RELW = STEPS + SPR
    assert o <= X * HC * DO - RELW
    rel, _ = at(region, X * HC * DO - RELW, RELW)
    grow, o = at(region, 0, SPR, GW)
    hot_a, o = at(region, o, HALF, P)
    hot_b, o = at(region, o, SPR - HALF, P)
    assert o <= X * HC * DO - RELW
    w2_sb = region[:, :].rearrange("p (e k o) -> p e k o", e=X, k=HC)
    iota_i, o = at(pay_flat, 0, STEPS)
    iota_f, o = at(pay_flat, o, STEPS)
    srcs, o = at(pay_flat, o, RELW)
    iota_i, srcs = iota_i.bitcast(I32), srcs.bitcast(I32)
    wg_sb, o = at(pay_flat, o, 2, 2 * D)
    assert o <= 2 * B * ROW
    pad_i = pairbuf[:, 0:4, :].rearrange("p a b -> p (a b)")[0:1, 0:8 * P].rearrange("p (a b) -> p a b", a=2).bitcast(I32)
    b1_row, _ = at(acc, NT * GW - X * H, X, H)
    BUSY = X * H // GW + 1

    psum = [nc.alloc_psum_tensor(f"psum{n}", [P, 512], F32) for n in range(8)]

    def sem(name):
        return nc.alloc_semaphore(name)

    c_dve = Chain(nc, "c_dve")
    c_dve.begin()
    c_dve.per = 0
    c_pool = Chain(nc, "c_pool")
    c_pool.begin()
    c_pool.per = 0
    c_pe = Chain(nc, "c_pe")
    c_pe.begin()
    c_pe.per = 0
    c_act = Chain(nc, "c_act")
    c_act.begin()
    c_act.per = 0

    s_edges, s_fst, s_small, s_gw, s_x, s_w1 = (sem(n) for n in ("s_edges", "s_fst", "s_small", "s_gw", "s_x", "s_w1"))
    act.dma_start(src_tab[0:E], src[:]).then_inc(s_edges, 16)
    act.dma_start(dst_tab[0:E], dst[:]).then_inc(s_edges, 16)
    act.dma_start(fst_i[0:1, :], dst[P:E:P].unsqueeze(0), allow_slow_non_contiguous=True).then_inc(s_fst, 16)
    act.dma_start(wg_sb[:, :, :], gnn_w.rearrange("(o p) i -> p o i", p=P)).then_inc(s_gw, 16)
    act.dma_start(gb_row[:, :], gnn_b.unsqueeze(0)).then_inc(s_small, 16)
    act.dma_start(gam[:, :], gamma.rearrange("(c p) -> p c", p=P), allow_slow_non_contiguous=True).then_inc(s_small, 16)
    act.dma_start(bet[:, :], beta.rearrange("(c p) -> p c", p=P), allow_slow_non_contiguous=True).then_inc(s_small, 16)
    act.dma_start(wr_sb[:, :, :], wr.rearrange("(c p) e -> p c e", p=P)).then_inc(s_small, 16)
    act.dma_start(br_row[:, :], br.unsqueeze(0)).then_inc(s_small, 16)

    pool.iota(iota_i, [[1, STEPS]], channel_multiplier=0)
    t_iota = c_pool.inc(pool.iota(pcol_i[:, :], [[0, 1]], channel_multiplier=1))
    PADN = TABLE * P - E
    dve.memset(pad_i[:, 0, :], 0)
    t_pad = c_dve.inc(dve.memset(pad_i[:, 1, :], 2 * NT * P))
    c_dve.wait(sp, t_pad)
    sp.dma_start(src_tab[E:E + PADN].unsqueeze(0), pad_i[:, 0, 0:PADN]).then_inc(s_edges, 16)
    sp.dma_start(dst_tab[E:E + PADN].unsqueeze(0), pad_i[:, 1, 0:PADN]).then_inc(s_edges, 16)
    t_tail = c_dve.inc(dve.memset(xall[96:P, NT - 1, :], 0.0))
    dve.memset(ones[:, :], 1.0)
    dve.memset(ones_b[:, :], 1.0)
    c_pool.wait(dve, t_iota)
    dve.tensor_copy(iota[:, :], iota_i[:, 0:P])
    dve.tensor_copy(iota_f, iota_i)
    c_dve.then(dve, dve.tensor_copy(pcol[:, :], pcol_i[:, :]))
    dve.tensor_scalar(ident[:, :], iota[:, :], pcol[:, 0:1], None, ALU.is_equal)
    bound = sb("bound", [P, 1])
    dve.tensor_scalar(bound[:, :], pcol[:, :], float(P), float(P), ALU.mult, ALU.add)
    t_const = c_dve.inc(dve.tensor_scalar(tri_b[:, :], iota[:, :], pcol[:, 0:1], None, ALU.is_gt))

    dve.wait_ge(s_fst, 16)
    t_fst = c_dve.inc(dve.tensor_copy(fst_f[0:1, :], fst_i[0:1, :]))
    c_dve.wait(pe, t_fst)
    pe.matmul(psum[0][0:NT, 0:512], ones[0:1, 0:NT], fst_f[0:1, 0:512], start=True, stop=True)
    t = c_pe.inc(pe.matmul(psum[1][0:NT, 0:FIRSTS - 512], ones[0:1, 0:NT], fst_f[0:1, 512:FIRSTS], start=True, stop=True))
    c_pe.wait(dve, t)
    c_dve.wait(dve, t_const)
    dve.tensor_scalar(below[0:NT, 0:512], psum[0][0:NT, 0:512], bound[0:NT, 0:1], None, ALU.is_lt)
    c_dve.then(dve, dve.tensor_scalar(below[0:NT, 512:FIRSTS], psum[1][0:NT, 0:FIRSTS - 512], bound[0:NT, 0:1], None, ALU.is_lt))
    key = sb("key", [P, 1])
    c_dve.then(dve, dve.tensor_reduce(key[0:NT, :], below[0:NT, :], AX_X, ALU.add))
    c_dve.then(dve, dve.tensor_tensor(key[0:NT, :], key[0:NT, :], pcol[0:NT, :], ALU.add))
    t = c_dve.inc(dve.tensor_scalar(passed[0:NT, :], iota_f[0:NT, :], key[0:NT, 0:1], None, ALU.is_gt))
    c_dve.wait(pe, t)
    pe.matmul(psum[0][0:1, 0:512], ones[0:NT, 0:1], passed[0:NT, 0:512], start=True, stop=True)
    pe.matmul(psum[1][0:1, 0:STEPS - 512], ones[0:NT, 0:1], passed[0:NT, 512:STEPS], start=True, stop=True)
    for b in range(B):
        m = pe.matmul(psum[2][0:SB, b:b + 1], passed[0:NT, b * SB:(b + 1) * SB], ones[0:NT, 0:1], start=True, stop=True)
    t = c_pe.inc(m)
    c_pe.wait(dve, t)
    last = float(NT - 1)
    dve.tensor_scalar(n_row[0:1, 0:512], psum[0][0:1, 0:512], last, None, ALU.min)
    t_nrow = c_dve.inc(dve.tensor_scalar(n_row[0:1, 512:STEPS], psum[1][0:1, 0:STEPS - 512], last, None, ALU.min))
    n_col, step_col, e_col, e_idx = sb("n_col", [P, B]), sb("step_col", [P, B]), sb("e_col", [P, B]), sb("e_idx", [P, B], I32)
    step_i = sb("step_i", [P, B], I32)
    t = c_pool.inc(pool.iota(step_i[:, :], [[SB, B]], channel_multiplier=1))
    c_pool.wait(dve, t)
    dve.tensor_copy(step_col[:, :], step_i[:, :])
    c_dve.then(dve, dve.tensor_scalar(n_col[0:SB, :], psum[2][0:SB, 0:B], last, None, ALU.min))
    c_dve.then(dve, dve.tensor_tensor(e_col[0:SB, :], step_col[0:SB, :], n_col[0:SB, :], ALU.subtract))
    t = c_dve.inc(dve.tensor_copy(e_idx[0:SB, :], e_col[0:SB, :]))
    c_dve.then(dve, dve.tensor_scalar(n_col[0:SB, :], n_col[0:SB, :], float(P), None, ALU.mult))
    c_dve.wait(pool, t)
    pool.wait_ge(s_edges, 64)
    s_tab = sem("s_tab")
    for k, tab in enumerate((src_tab, dst_tab)):
        tiles = tab.rearrange("(a b) -> a b", b=P)
        for b in range(B):
            pool.indirect_dma_start(tab_i[0:SB, k * B + b, :], None, tiles,
                                    bass.IndirectOffsetOnAxis(e_idx[0:SB, b:b + 1], 0)).then_inc(s_tab, 16)

    s_h = sem("s_h")
    ln = Chain(nc, "ln_dve", per=5)
    ln_sd = Event(nc, "ln_sd")
    ln_h = Event(nc, "ln_h")

    def load_x(b):
        if isinstance(b, int) and b == NB - 1:
            c_dve.wait(sp, t_tail)
            t0 = b * B
            sp.dma_start(xall[:, t0:NT - 1, :], x[t0 * P:(NT - 1) * P, :].rearrange("(t p) d -> p t d", p=P)).then_inc(s_x, 16)
            sp.dma_start(xall[0:TAIL, NT - 1, :], x[(NT - 1) * P:N, :]).then_inc(s_x, 16)
        else:
            sp.dma_start(xall[:, ds(b * B, B), :], x[ds(b * (B * P), B * P), :].rearrange("(t p) d -> p t d", p=P)).then_inc(s_x, 16)
            landed = sp.to_reg(b * 16 + 16)
            sp.wait_ge(s_x, 16)
            sp.wait_ge(s_x, landed)

    def norm(b, x_count):
        if not isinstance(b, int):
            x_count = dve.to_reg(x_count)
        dve.wait_ge(s_x, 16)
        dve.wait_ge(s_x, x_count)
        ln.begin(b)
        for j in range(B):
            i = dve.bn_stats(stats[:, j, :], xall[:, ds(b * B + j, 1), :].rearrange("p a d -> p (a d)"))
        ln.then(dve, i, apart=True)
        for j in range(B):
            i = dve.bn_aggr(mv[:, j, :], stats[:, j, :])
        ln.then(dve, i)
        means, variances = mv[:, :, 0], mv[:, :, 1]
        t = ln.inc(dve.tensor_scalar(sd[:, :], variances, EPS, None, ALU.add))
        ln.wait(act, t, b)
        ln_sd.inc(act.activation(sd[:, :], sd[:, :], ACT.Sqrt))
        ln_sd.wait(dve, 1, b)
        r = rstd[:, ds(b * B, B)]
        ln.then(dve, dve.reciprocal(r, sd[:, :]))
        t = ln.inc(dve.scalar_tensor_tensor(nmr[:, ds(b * B, B)], means, -1.0, r, ALU.mult, ALU.mult))
        ln.end()
        ln.wait(act, t, b)
        for j in range(B):
            i = act.activation(acc3[:, ds(b * B + j, 1), 0:D], xall[:, ds(b * B + j, 1), :], ACT.Identity,
                               bias=nmr[:, ds(b * B + j, 1)], scale=rstd[:, ds(b * B + j, 1)])
        ln_h.inc(i)
        ln_h.wait(act, 1, b)
        act.dma_start(h_rows[ds(b * (B * P), B * P), :].rearrange("(t p) d -> p t d", p=P),
                      acc3[:, ds(b * B, B), 0:D]).then_inc(s_h, 16)

    with nc.Fori(0, NB - 1) as b:
        load_x(b)
        norm(b, b * 16 + 16)
    load_x(NB - 1)
    for e in range(X):
        sp.dma_start(w1_sb[:, e, :, :], w1[e].rearrange("(c p) h -> p c h", p=P)).then_inc(s_w1, 16)
    norm(NB - 1, NB * 16 + 16)
    sp.wait_ge(s_h, 16 * NB)
    sp.dma_start(b1_row[0:1, :, :], b1.unsqueeze(0)).then_inc(s_w1, 16)

    dve.wait_ge(s_tab, 16 * 2 * B)
    t_rel = None
    for b in range(B):
        dve.tensor_copy(tab_f[0:SB, b, :], tab_i[0:SB, b, :])
        i = dve.tensor_scalar(tab_f[0:SB, B + b, :], tab_i[0:SB, B + b, :], n_col[0:SB, b:b + 1], None, ALU.subtract)
    dve.memset(rel[:, STEPS:RELW], -1.0)
    t = c_dve.inc(dve.memset(srcs[:, STEPS:RELW], 0))
    c_dve.wait(pe, t)
    groups = [(0, 4), (4, B)]
    for k in range(2):
        for g, (lo, hi) in enumerate(groups):
            for b in range(lo, hi):
                i = pe.transpose(psum[2 * k + g][:, (b - lo) * SB:(b - lo + 1) * SB], tab_f[0:SB, k * B + b, :], ident[0:SB, 0:SB])
    t = c_pe.inc(i)
    c_pe.wait(dve, t)
    for g, (lo, hi) in enumerate(groups):
        dve.tensor_copy(srcs[:, lo * SB:hi * SB], psum[g][:, 0:(hi - lo) * SB])
        i = dve.tensor_copy(rel[:, lo * SB:hi * SB], psum[2 + g][:, 0:(hi - lo) * SB])
    t_rel = c_dve.inc(i)

    pe.wait_ge(s_gw, 16)
    for c in range(2 * DC):
        for o_ in range(2):
            i = pe.transpose(psum[4 + c // 2][:, (c % 2) * D + o_ * P:(c % 2) * D + (o_ + 1) * P],
                             wg_sb[:, o_, c * P:(c + 1) * P], ident[:, :])
    t = c_pe.inc(i)
    c_pe.wait(dve, t)
    for g in range(DC):
        i = dve.tensor_copy(wgt[:, 2 * g:2 * g + 2, :].rearrange("p a b -> p (a b)"), psum[4 + g][:, :])
    t_wgt = c_dve.inc(i)

    dve.wait_ge(s_small, 16 * 5)
    pe.wait_ge(s_w1, 16 * (X + 1))
    pe.wait_ge(s_small, 16 * 5)
    for c in range(DC):
        pe.matmul(psum[6][0:1, 0:X], bet[:, c:c + 1], wr_sb[:, c, :], start=(c == 0), stop=False)
    t = c_pe.inc(pe.matmul(psum[6][0:1, 0:X], ones[0:1, 0:1], br_row[0:1, :], start=False, stop=True))
    c_pe.wait(dve, t)
    dve.tensor_copy(br_row[0:1, :], psum[6][0:1, 0:X])
    for c in range(DC):
        i = dve.tensor_scalar(wr_sb[:, c, :], wr_sb[:, c, :], gam[:, c:c + 1], None, ALU.mult)
    t_wr = c_dve.inc(i)
    evac = []
    for e in range(X):
        bank = psum[6 + e % 2]
        if e >= 2:
            c_act.wait(pe, evac[e - 2])
        elif e == 0:
            c_dve.wait(pe, t_wr)
        for c in range(DC):
            pe.matmul(bank[0:1, :], bet[:, c:c + 1], w1_sb[:, e, c, :], start=(c == 0), stop=False)
        t = c_pe.inc(pe.matmul(bank[0:1, :], ones[0:1, 0:1], b1_row[0:1, e, :], start=False, stop=True))
        c_pe.wait(act, t)
        evac.append(c_act.inc(act.copy(b1_row[0:1, e, :], bank[0:1, :])))
        for c in range(DC):
            act.mul(w1_sb[:, e, c, :], w1_sb[:, e, c, :], gam[:, c:c + 1])

    s_b1 = sem("s_b1")
    c_act.wait(sp, evac[-1])
    sp.dma_start(b1_new.unsqueeze(0), b1_row[0:1, :, :]).then_inc(s_b1, 16)

    step_mm = Event(nc, "step_mm", SPR, credit_by=pe)
    step_add = Event(nc, "step_add", SPR, credit_by=dve)
    hot_a_up = Event(nc, "hot_a_up")
    hot_b_up = Event(nc, "hot_b_up")
    idx_a_up = Event(nc, "idx_a_up")
    idx_b_up = Event(nc, "idx_b_up")
    own_h = Event(nc, "own_h")
    own_tr = Event(nc, "own_tr")
    own_cp = Event(nc, "own_cp")
    own_mm = Event(nc, "own_mm")
    own_add = Event(nc, "own_add", credit_by=dve)
    got = [sem(f"got{k}") for k in range(SPR)]
    BANKS = 4

    def one_hot(out_t, first, n):
        return dve.tensor_tensor(out_t, iota[:, :].unsqueeze(1).broadcast_to([P, n, P]),
                                 rel[:, ds(first, n)].unsqueeze(2).broadcast_to([P, n, P]), ALU.is_equal)

    c_dve.wait(dve, t_rel)
    dve.memset(grow[:, :, D:GW], 1.0)
    hot_a_up.inc(one_hot(hot_a, 0, HALF))
    dve.wait_ge(s_h, 16 * NB)
    t_ones = c_dve.inc(dve.memset(acc[:, 0:(NT - BUSY) * GW], 0.0))
    dve.wait_ge(s_b1, 16)
    t_zeros = c_dve.inc(dve.memset(acc[:, (NT - BUSY) * GW:], 0.0))
    c_dve.wait(act, t_rel)
    idx_a_up.inc(act.copy(idx_a[:, :], srcs[:, 0:HALF]))
    idx_b_up.inc(act.copy(idx_b[:, :], srcs[:, HALF:SPR]))
    c_dve.wait(dve, t_nrow)
    c_dve.wait(dve, t_zeros)
    c_dve.wait(pe, t_ones)
    c_dve.wait(pool, t_ones)
    pool.wait_ge(s_h, 16 * NB)

    act.wait_ge(s_edges, 64)

    with nc.Fori(0, NT) as r:
        first = r * SPR
        hot_a_free, hot_b_free = HALF, SPR
        step_mm.wait(dve, hot_b_free, r, back=1)
        hot_b_up.inc(one_hot(hot_b, first + HALF, SPR - HALF))
        own_h.inc(act.activation(rowsb[:, 0, :], xall[:, ds(r, 1), :].rearrange("p a d -> p (a d)"), ACT.Identity,
                                 bias=nmr[:, ds(r, 1)], scale=rstd[:, ds(r, 1)]))
        for k in range(SPR):
            if k in (0, HALF):
                (idx_a_up if k < HALF else idx_b_up).wait(pool, 1, r)
            step_mm.wait(pool, k + 1, r, back=1, apart=True)
            idx = idx_a[:, k:k + 1] if k < HALF else idx_b[:, k - HALF:k - HALF + 1]
            pool.indirect_dma_start(grow[:, k, 0:D], None, h_rows, bass.IndirectOffsetOnAxis(idx, 0)).then_inc(got[k], 16)
            bank = psum[k % BANKS]
            pe.wait_ge(got[k], r * 16 + 16)
            if k == 0:
                hot_a_up.wait(pe, 1, r)
            if k == HALF:
                hot_b_up.wait(pe, 1, r)
            if k >= BANKS:
                step_add.wait(pe, k - BANKS + 1, r)
            else:
                step_add.wait(pe, max(q for q in range(SPR) if q % BANKS == k) + 1, r, back=1)
            hot = hot_a[:, k, :] if k < HALF else hot_b[:, k - HALF, :]
            step_mm.inc(pe.matmul(bank[:, 0:GW], hot, grow[:, k, :], start=True, stop=True))
            window = dve.value_load(n_row[0:1, ds(first + k, 1)], min_val=0, max_val=NT - 1)
            sums = acc3[:, ds(window, 1), :].rearrange("p a c -> p (a c)")
            step_mm.wait(dve, k + 1, r)
            if k:
                step_add.wait(dve, k, r)
            else:
                step_add.wait(dve, SPR, r, back=1)
            step_add.inc(dve.tensor_tensor(sums, sums, bank[:, 0:GW], ALU.add))
            if k == 2:
                own_h.wait(pe, 1, r)
                for c in range(DC):
                    i = pe.transpose(psum[4][:, c * P:(c + 1) * P], rowsb[:, 0, c * P:(c + 1) * P], ident[:, :])
                own_tr.inc(i)
                own_tr.wait(act, 1, r)
                own_cp.inc(act.copy(trsb[:, 0, :], psum[4][:, 0:D]))
            if k == 6:
                own_cp.wait(pe, 1, r)
                own_add.wait(pe, 1, r, back=1)
                for c in range(DC):
                    pe.matmul(psum[5][:, 0:D], trsb[:, 0, c * P:(c + 1) * P], wgt[:, c, :], start=(c == 0), stop=False)
                own_mm.inc(pe.matmul(psum[5][:, 0:D], ones[0:1, :], gb_row[0:1, :], start=False, stop=True))
            if k == HALF - 1:
                step_mm.wait(dve, HALF, r)
                hot_a_up.inc(one_hot(hot_a, first + SPR, HALF))
                step_mm.wait(act, HALF, r)
                idx_a_up.inc(act.copy(idx_a[:, :], srcs[:, ds(first + SPR, HALF)]))
            if k == HALF:
                own_mm.wait(dve, 1, r)
                xt = xall[:, ds(r, 1), :].rearrange("p a d -> p (a d)")
                own_add.inc(dve.tensor_tensor(xt, xt, psum[5][:, 0:D], ALU.add))
        step_mm.wait(act, SPR, r)
        idx_b_up.inc(act.copy(idx_b[:, :], srcs[:, ds(first + SPR + HALF, SPR - HALF)]))

    s_w2 = sem("s_w2")
    step_mm.wait(sp, SPR, NT - 1)
    step_add.wait(sp, SPR, NT - 1)
    hot_a_up.wait(sp, 1, NT)
    for e in range(X):
        sp.dma_start(w2_sb[:, e, :, :], w2[e].rearrange("(k p) o -> p k o", p=P)).then_inc(s_w2, 16)

    rdeg = sb("rdeg", [P, NT])
    valid = sb("valid", [P, NT])
    tok = sb("tok", [P, NT])
    trash = sb("trash", [P, 2, NT])
    tok_i = sb("tok_i", [P, NT], I32)
    carry = sb("carry", [P, X])
    qbase = sb("qbase", [P, X])
    qbase_i = sb("qbase_i", [P, X], I32)
    s_out = sem("s_out")
    c_pool2 = Chain(nc, "c_pool2")
    c_pool2.begin()
    pool.iota(tok_i[:, :], [[P, NT]], channel_multiplier=1)
    t = c_pool2.inc(pool.iota(qbase_i[:, :], [[QUEUE, X]], channel_multiplier=0))
    c_pool2.wait(dve, t)
    c2 = Chain(nc, "c2")
    c2.begin()
    step_add.wait(dve, SPR, NT - 1)
    dve.tensor_copy(tok[:, :], tok_i[:, :])
    dve.tensor_copy(qbase[:, :], qbase_i[:, :])
    c2.then(dve, dve.tensor_scalar(rdeg[:, :], acc3[:, :, D:GW].rearrange("p a o -> p (a o)"), 1.0, None, ALU.max))
    c2.then(dve, dve.reciprocal(rdeg[:, :], rdeg[:, :]))
    dve.tensor_copy(carry[:, :], qbase[:, :])
    c2.then(dve, dve.tensor_scalar(valid[:, :], tok[:, :], float(N), None, ALU.is_lt))
    c2.then(dve, dve.tensor_scalar(trash[:, 1, :], valid[:, :], -1.0, 1.0, ALU.mult, ALU.add))
    c2.then(dve, dve.tensor_scalar(bound[:, :], pcol[:, :], float(TRASH), None, ALU.add))
    c2.then(dve, dve.tensor_scalar(trash[:, 0, :], trash[:, 1, :], bound[:, 0:1], None, ALU.mult))
    t_rt = c2.then(dve, dve.scalar_tensor_tensor(trash[:, 1, :], trash[:, 1, :], float(P), trash[:, 0, :], ALU.mult, ALU.add))
    zero = sb("zero", [P, D])
    t_zero = c2.inc(dve.memset(zero[:, :], 0.0))
    c2.wait(sp, t_zero)
    sp.dma_start(out[NT * P:NT * P + P, :], zero[:, :]).then_inc(s_out, 16)
    c2.wait(act, t_rt)

    small = sb("small", [P, 12, B])
    var1, sd1, r1, u1, sd2, r2, rr, nm, dif, ex, wa, wb = (small[:, n, :] for n in range(12))
    lg = sb("lg", [P, B, X])
    top = sb("top", [P, B, X])
    topi = sb("topi", [P, B, X], U32)
    e12 = sb("e12", [P, B, 2])
    pick1 = sb("pick1", [P, B, X])
    pick2 = sb("pick2", [P, B, X])
    both = sb("both", [P, B, X], BF16)
    both_f = sb("both_f", [P, B, X])
    rank = sb("rank", [P, B, X])
    prod = sb("prod", [P, B, X])
    slot = sb("slot", [P, 2, B])
    slot_i = sb("slot_i", [P, 2, 2, B], I32)
    total = sb("total", [P, X])

    g_am = Event(nc, "g_am", B)
    g_ta = Event(nc, "g_ta", B)
    g_at = Event(nc, "g_at", B)
    g_mm = Event(nc, "g_mm", B)
    g_x1 = Event(nc, "g_x1", B)
    g_sq = Event(nc, "g_sq", 2)
    g_xh = Event(nc, "g_xh")
    g_tx = Event(nc, "g_tx", B)
    g_xt = Event(nc, "g_xt", B)
    g_lg = Event(nc, "g_lg")
    g_ex = Event(nc, "g_ex")
    g_rk = Event(nc, "g_rk")
    g_sc = Event(nc, "g_sc", credit_by=pool)
    g_sc.credit = 2
    pool.sem_inc(g_sc.sem, 1)
    s_sc = sem("s_sc")
    ch = Chain(nc, "router_dve", per=34)

    def router(b, par):
        ch.begin(b)
        tile = lambda v, j: v[:, ds(b * B + j, 1), :].rearrange("p a d -> p (a d)")
        for j in range(B + 1):
            if j < B:
                if j >= 2:
                    g_ta.wait(act, j - 1, b)
                g_am.inc(act.mul(rowsb[:, j % 2, :], acc3[:, ds(b * B + j, 1), 0:D].rearrange("p a d -> p (a d)"),
                                 rdeg[:, ds(b * B + j, 1)]))
                g_am.wait(pe, j + 1, b)
                if j >= 2:
                    g_at.wait(pe, j - 1, b)
                for c in range(DC):
                    i = pe.transpose(psum[j % 2][:, c * P:(c + 1) * P], rowsb[:, j % 2, c * P:(c + 1) * P], ident[:, :])
                g_ta.inc(i)
                if j >= 2:
                    g_mm.wait(act, j - 1, b)
                g_ta.wait(act, j + 1, b)
                g_at.inc(act.copy(trsb[:, j % 2, :], psum[j % 2][:, 0:D]))
            if j >= 1:
                q = j - 1
                g_at.wait(pe, q + 1, b)
                if q >= 2:
                    g_x1.wait(pe, q - 1, b)
                for c in range(DC):
                    i = pe.matmul(psum[2 + q % 2][:, 0:D], trsb[:, q % 2, c * P:(c + 1) * P], wgt[:, DC + c, :],
                                  start=(c == 0), stop=(c == DC - 1))
                g_mm.inc(i)
                g_mm.wait(dve, q + 1, b)
                g_x1.inc(dve.tensor_tensor(tile(xall, q), tile(xall, q), psum[2 + q % 2][:, 0:D], ALU.add))
                if q >= 1:
                    g_x1.wait(dve, q, b, apart=True)
                    dve.bn_stats(stats[:, q - 1, :], tile(xall, q - 1))
        g_x1.wait(dve, B, b, apart=True)
        ch.then(dve, dve.bn_stats(stats[:, B - 1, :], tile(xall, B - 1)), apart=True)
        g_x1.wait(sp, B, b)
        sp.dma_start(out[ds(b * (B * P), B * P), :].rearrange("(t p) d -> p t d", p=P), xall[:, ds(b * B, B), :]).then_inc(s_out, 16)
        for j in range(B):
            i = dve.bn_aggr(mv[:, j, :], stats[:, j, :])
        ch.then(dve, i)
        mean, var = mv[:, :, 0], mv[:, :, 1]
        t = ch.inc(dve.tensor_scalar(var1, var, EPS, None, ALU.add))
        ch.wait(act, t, b)
        g_sq.inc(act.activation(sd1, var1, ACT.Sqrt))
        g_sq.wait(dve, 1, b)
        ch.then(dve, dve.reciprocal(r1, sd1))
        ch.then(dve, dve.tensor_tensor(u1, var, r1, ALU.mult))
        ch.then(dve, dve.tensor_tensor(u1, u1, r1, ALU.mult))
        t = ch.inc(dve.tensor_scalar(u1, u1, EPS, None, ALU.add))
        ch.wait(act, t, b)
        g_sq.inc(act.activation(sd2, u1, ACT.Sqrt))
        g_sq.wait(dve, 2, b)
        ch.then(dve, dve.reciprocal(r2, sd2))
        ch.then(dve, dve.tensor_tensor(rr, r1, r2, ALU.mult))
        t = ch.inc(dve.scalar_tensor_tensor(nm, mean, -1.0, rr, ALU.mult, ALU.mult))
        ch.wait(act, t, b)
        g_sc.wait(act, 1, b, back=2)
        for j in range(B):
            i = act.activation(pay[:, par, j, 0:D], tile(xall, j), ACT.Identity, bias=nm[:, j:j + 1], scale=rr[:, j:j + 1])
        g_xh.inc(i)
        g_xh.wait(pe, 1, b)
        for j in range(B):
            if j >= 2:
                g_xt.wait(pe, j - 1, b)
            for c in range(DC):
                i = pe.transpose(psum[j % 2][:, c * P:(c + 1) * P], pay[:, par, j, c * P:(c + 1) * P], ident[:, :])
            g_tx.inc(i)
            g_tx.wait(act, j + 1, b)
            if j >= 2:
                g_lg.wait(act, j - 1, b)
            g_xt.inc(act.copy(trsb[:, j % 2, :], psum[j % 2][:, 0:D]))
            g_xt.wait(pe, j + 1, b)
            cols = psum[4][:, j * X:(j + 1) * X]
            for c in range(DC):
                pe.matmul(cols, trsb[:, j % 2, c * P:(c + 1) * P], wr_sb[:, c, :], start=(c == 0), stop=False)
            g_lg.inc(pe.matmul(cols, ones[0:1, :], br_row[0:1, :], start=False, stop=True))
        g_lg.wait(dve, B, b)
        ch.then(dve, dve.tensor_copy(lg[:, :, :].rearrange("p a b -> p (a b)"), psum[4][:, 0:B * X]), apart=True)
        for j in range(B):
            i = dve.max(top[:, j, :], lg[:, j, :])
        ch.then(dve, i, apart=True)
        for j in range(B):
            i = dve.max_index(topi[:, j, :], top[:, j, :], lg[:, j, :])
        t = ch.inc(dve.tensor_tensor(dif, top[:, :, 1], top[:, :, 0], ALU.subtract))
        ch.wait(act, t, b)
        g_ex.inc(act.activation(ex, dif, ACT.Exp))
        ch.wait(dve, t, b)
        ch.then(dve, dve.tensor_copy(e12[:, :, :], topi[:, :, 0:2]))
        io8 = iota[:, 0:X].unsqueeze(1).broadcast_to([P, B, X])
        dve.tensor_tensor(pick1[:, :, :], io8, e12[:, :, 0:1].broadcast_to([P, B, X]), ALU.is_equal)
        ch.then(dve, dve.tensor_tensor(pick2[:, :, :], io8, e12[:, :, 1:2].broadcast_to([P, B, X]), ALU.is_equal))
        ch.then(dve, dve.tensor_tensor(both_f[:, :, :], pick1[:, :, :], pick2[:, :, :], ALU.add))
        vb = valid[:, ds(b * B, B)]
        t = ch.inc(dve.tensor_tensor(both[:, :, :], both_f[:, :, :], vb.unsqueeze(2).broadcast_to([P, B, X]), ALU.mult))
        ch.wait(pe, t, b)
        rk = psum[5][:, 0:B * X].rearrange("p (a b) -> p a b", a=B)
        pe.matmul(rk, tri_b[:, :], both[:, :, :], start=True, stop=True)
        for j in range(B - 1):
            pe.matmul(rk[:, j + 1:B, :], ones_b[:, :], both[:, j:j + 1, :].broadcast_to([P, B - 1 - j, X]),
                      start=False, stop=True, skip_group_check=True)
        g_rk.inc(pe.matmul(psum[6][:, 0:B * X].rearrange("p (a b) -> p a b", a=B), ones_b[:, :], both[:, :, :], start=True, stop=True))
        g_ex.wait(dve, 1, b)
        ch.then(dve, dve.tensor_scalar(wa, ex, 1.0, None, ALU.add))
        ch.then(dve, dve.reciprocal(wa, wa))
        ch.then(dve, dve.tensor_tensor(wb, ex, wa, ALU.mult), apart=True)
        rows = pay[:, par, :, :]
        dve.tensor_copy(rows[:, :, D:D + 1], tok[:, ds(b * B, B)].unsqueeze(2))
        dve.tensor_copy(rows[:, :, D + 1:D + 2], e12[:, :, 0:1])
        dve.tensor_tensor(rows[:, :, D + 2:D + 3], wa.unsqueeze(2), wb.unsqueeze(2), ALU.subtract)
        ch.inc(dve.tensor_copy(rows[:, :, D + 3:D + 4], wb.unsqueeze(2)))
        g_rk.wait(dve, 1, b)
        ch.then(dve, dve.tensor_tensor(rank[:, :, :], rk, carry[:, :].unsqueeze(1).broadcast_to([P, B, X]), ALU.add))
        ch.then(dve, dve.tensor_reduce(total[:, :], psum[6][:, 0:B * X].rearrange("p (a b) -> p b a", a=B), AX_X, ALU.add))
        ch.then(dve, dve.tensor_tensor(carry[:, :], carry[:, :], total[:, :], ALU.add))
        for s, pick in enumerate((pick1, pick2)):
            ch.then(dve, dve.tensor_tensor(prod[:, :, :], rank[:, :, :], pick[:, :, :], ALU.mult))
            ch.then(dve, dve.tensor_reduce(slot[:, s, :], prod[:, :, :], AX_X, ALU.add))
            ch.then(dve, dve.tensor_tensor(slot[:, s, :], slot[:, s, :], vb, ALU.mult))
            ch.then(dve, dve.tensor_tensor(slot[:, s, :], slot[:, s, :], trash[:, s, ds(b * B, B)], ALU.add))
            t = ch.then(dve, dve.tensor_scalar(slot_i[:, par, s, :], slot[:, s, :], 0.0, None, ALU.add))
        ch.end()
        ch.wait(pool, t, b)
        g_xh.wait(pool, 1, b, apart=True)
        for j in range(B):
            for s in range(2):
                pool.indirect_dma_start(queue, bass.IndirectOffsetOnAxis(slot_i[:, par, s, j:j + 1], 0),
                                        pay[:, par, j, :], None).then_inc(s_sc, 16)
        pool.wait_ge(s_sc, b * (16 * 2 * B) + 16 * 2 * B)
        pool.sem_inc(g_sc.sem, 1)

    g_lg.per = B
    with nc.Fori(0, NB // 2) as r:
        router(r * 2, 0)
        router(r * 2 + 1, 1)
    router(NB - 1, 0)

    b2_bc, o = at(acc, 0, X, DO)
    b1_bc, o = at(acc, o, X, H)
    qrow = [None, None]
    xt, hid, gel, ysb = [None] * 2, [None] * 2, [None] * 2, [None] * 2
    for p_ in range(2):
        qrow[p_], o = at(acc, o, ROW)
        xt[p_], o = at(acc, o, D)
        hid[p_], o = at(acc, o, H)
        gel[p_], o = at(acc, o, H)
        ysb[p_], o = at(acc, o, DO)
    ge, o = at(acc, o, QT, X)
    gt, o = at(acc, o, QT, X)
    eq_, o = at(acc, o, QT)
    begin, o = at(acc, o, QT)
    live, o = at(acc, o, QT)
    off_i, o = at(acc, o, QT)
    ew_i, o = at(acc, o, QT)
    wcol, o = at(acc, o, QT)
    tokens, o = at(acc, o, QT)
    off_i, ew_i = off_i.bitcast(I32), ew_i.bitcast(I32)
    assert o <= NT * GW and QT <= P
    padrow = sb("padrow", [P, ROW])
    cnt, cnt_i, tls, cum = sb("cnt", [P, X]), sb("cnt_i", [P, X], I32), sb("tls", [P, X]), sb("cum", [P, X])
    pslot_i = sb("pslot_i", [P, X], I32)

    g_xt.wait(sp, B, NB - 1)
    s_b2 = sem("s_b2")
    sp.dma_start(b1_bc, b1_new.unsqueeze(0).broadcast_to([P, X, H])).then_inc(s_b2, 16)
    sp.dma_start(b2_bc, b2.unsqueeze(0).broadcast_to([P, X, DO])).then_inc(s_b2, 16)

    c3 = Chain(nc, "c3")
    c3.begin()
    c3.then(dve, dve.memset(padrow[:, :], 0.0))
    c3.then(dve, dve.memset(padrow[:, D + 1:D + 2], -1.0))
    c3.then(dve, dve.tensor_scalar(padrow[:, D:D + 1], pcol[:, :], float(N), None, ALU.add))
    c3.then(dve, dve.tensor_scalar(cnt[:, :], carry[:, :], pcol[:, 0:1], None, ALU.add))
    t_pad = c3.then(dve, dve.tensor_copy(pslot_i[:, :], cnt[:, :]))
    c3.wait(pool, t_pad)
    s_pad, s_idle = sem("s_pad"), sem("s_idle")
    for e in range(X):
        pool.indirect_dma_start(queue, bass.IndirectOffsetOnAxis(pslot_i[:, e:e + 1], 0), padrow[:, :], None).then_inc(s_pad, 16)
    c3.wait(sp, t_pad)
    sp.dma_start(queue[IDLE:IDLE + P, :], padrow[:, :]).then_inc(s_idle, 16)
    c3.then(dve, dve.tensor_tensor(cnt[:, :], carry[:, :], qbase[:, :], ALU.subtract))
    c3.then(dve, dve.tensor_scalar(cnt_i[:, :], cnt[:, :], float(P - 1), None, ALU.add))
    c3.then(dve, dve.tensor_scalar(cnt_i[:, :], cnt_i[:, :], P.bit_length() - 1, None, ALU.arith_shift_right))
    c3.then(dve, dve.tensor_copy(tls[:, :], cnt_i[:, :]))
    c3.then(dve, dve.tensor_tensor_scan(cum[:, :], ones[:, 0:X], tls[:, :], 0.0, ALU.mult, ALU.add))
    jcol = iota[:, 0:QT]
    c3.then(dve, dve.tensor_tensor(ge, jcol.unsqueeze(2).broadcast_to([P, QT, X]), cum[:, :].unsqueeze(1).broadcast_to([P, QT, X]), ALU.is_ge))
    c3.then(dve, dve.tensor_tensor(gt, ge, tls[:, :].unsqueeze(1).broadcast_to([P, QT, X]), ALU.mult))
    dve.tensor_reduce(eq_, ge, AX_X, ALU.add)
    c3.then(dve, dve.tensor_reduce(begin, gt, AX_X, ALU.add))
    c3.then(dve, dve.tensor_scalar(live, eq_, float(X), float(P), ALU.is_lt, ALU.mult))
    c3.then(dve, dve.tensor_tensor(begin, jcol, begin, ALU.subtract))
    c3.then(dve, dve.tensor_tensor(begin, begin, live, ALU.mult))
    c3.then(dve, dve.scalar_tensor_tensor(off_i, eq_, float(QUEUE), begin, ALU.mult, ALU.add))
    t_tab = c3.then(dve, dve.tensor_scalar(ew_i, eq_, float(X - 1), None, ALU.min))
    c3.wait(sp, t_tab)
    c3.wait(pe, t_tab)
    c3.wait(dve, t_tab)
    sp.wait_ge(s_pad, 16 * X)
    sp.wait_ge(s_idle, 16)
    g_sc.wait(sp, 1, NB - 1)

    f_tx = Event(nc, "f_tx")
    f_xt = Event(nc, "f_xt")
    f_m1 = Event(nc, "f_m1")
    f_hb = Event(nc, "f_hb")
    f_th = Event(nc, "f_th")
    f_ge = Event(nc, "f_ge")
    f_m2 = Event(nc, "f_m2")
    f_w = Event(nc, "f_w")
    f_ys = Event(nc, "f_ys")
    f_sa = Event(nc, "f_sa", credit_by=pool)
    f_sa.credit = 2
    pool.sem_inc(f_sa.sem, 1)
    s_ld = [sem("s_ld0"), sem("s_ld1")]
    s_add = sem("s_add")
    w_chain = Chain(nc, "w_chain")
    y_chain = Chain(nc, "y_chain")
    tok_idx = sb("tok_idx", [P, 2], I32)
    XT, HID, HT, Y = (0, 1), (2, 3), (4, 5), (6, 7)

    def load_rows(j, par):
        row = sp.value_load(off_i[0:1, ds(j, 1)], min_val=0, max_val=IDLE)
        sp.dma_start(qrow[par], queue[ds(row, P), :]).then_inc(s_ld[par], 16)

    def rows_t(j, par, loads):
        pe.wait_ge(s_ld[par], loads)
        for c in range(DC):
            i = pe.transpose(psum[XT[par]][:, c * P:(c + 1) * P], qrow[par][:, c * P:(c + 1) * P], ident[:, :])
        f_tx.inc(i)
        f_tx.wait(dve, 1, j)
        f_xt.inc(dve.tensor_copy(xt[par], psum[XT[par]][:, 0:D]))

    def weights(j, par, loads):
        dve.wait_ge(s_ld[par], loads)
        dve.tensor_copy(tokens[:, ds(j, 1)], qrow[par][:, D:D + 1])
        w_chain.begin(j)
        w_chain.then(dve, dve.tensor_scalar(wcol[:, ds(j, 1)], qrow[par][:, D + 1:D + 2], eq_[:, ds(j, 1)],
                                            qrow[par][:, D + 2:D + 3], ALU.is_equal, ALU.mult))
        f_w.inc(dve.tensor_scalar(wcol[:, ds(j, 1)], wcol[:, ds(j, 1)], qrow[par][:, D + 3:D + 4], None, ALU.add))

    def layer1(j, par):
        expert = pe.value_load(ew_i[0:1, ds(j, 1)], min_val=0, max_val=X - 1)
        f_xt.wait(pe, 1, j)
        for c in range(DC):
            i = pe.matmul(psum[HID[par]][:, :], xt[par][:, c * P:(c + 1) * P],
                          w1_sb[:, ds(expert, 1), c, :].rearrange("p a h -> p (a h)"), start=(c == 0), stop=(c == DC - 1))
        f_m1.inc(i)

    def bias1(j, par):
        expert = dve.value_load(ew_i[0:1, ds(j, 1)], min_val=0, max_val=X - 1)
        f_m1.wait(dve, 1, j)
        f_hb.inc(dve.tensor_tensor(hid[par], psum[HID[par]][:, :],
                                   b1_bc[:, ds(expert, 1), :].rearrange("p a h -> p (a h)"), ALU.add))

    def next_load(j, par, after):
        f_w.wait(sp, 1, after)
        f_tx.wait(sp, 1, after, apart=True)
        load_rows(j, par)

    load_rows(0, 0)
    load_rows(1, 1)
    g_xt.wait(pe, B, NB - 1)
    g_rk.wait(pe, 1, NB - 1)
    ch.wait(pe, None, NB - 1)
    dve.wait_ge(s_b2, 32)
    for j in range(2):
        rows_t(j, j, 16)
        weights(j, j, 16)
        next_load(j + 2, j, j)
    layer1(0, 0)
    bias1(0, 0)
    pe.wait_ge(s_w2, 16 * X)
    pool.wait_ge(s_out, 16 * (NB + 1))

    with nc.Fori(0, PAIRS) as r:
        for par in range(2):
            j = r * 2 + par
            f_hb.wait(pe, 1, j)
            for k in range(HC):
                i = pe.transpose(psum[HT[par]][:, k * P:(k + 1) * P], hid[par][:, k * P:(k + 1) * P], ident[:, :])
            f_th.inc(i)
            f_th.wait(act, 1, j)
            f_ge.inc(act.activation(gel[par], psum[HT[par]][:, :], ACT.Gelu))
            layer1(j + 1, 1 - par)
            bias1(j + 1, 1 - par)
            rows_t(j + 2, par, r * 16 + 32)
            expert_p = pe.value_load(ew_i[0:1, ds(j, 1)], min_val=0, max_val=X - 1)
            f_ge.wait(pe, 1, j)
            for k in range(HC):
                i = pe.matmul(psum[Y[par]][:, 0:DO], gel[par][:, k * P:(k + 1) * P],
                              w2_sb[:, ds(expert_p, 1), k, :].rearrange("p a o -> p (a o)"), start=(k == 0), stop=(k == HC - 1))
            f_m2.inc(i)
            weights(j + 2, par, r * 16 + 32)
            next_load(j + 4, par, j + 2)
            expert_v = dve.value_load(ew_i[0:1, ds(j, 1)], min_val=0, max_val=X - 1)
            f_sa.wait(dve, 1, j, back=2)
            f_m2.wait(dve, 1, j)
            y_chain.begin(j)
            y_chain.then(dve, dve.tensor_tensor(ysb[par], psum[Y[par]][:, 0:DO],
                                                b2_bc[:, ds(expert_v, 1), :].rearrange("p a o -> p (a o)"), ALU.add))
            dve.tensor_copy(tok_idx[:, par:par + 1], tokens[:, ds(j, 1)])
            f_ys.inc(dve.tensor_scalar(ysb[par], ysb[par], wcol[:, ds(j, 1)], None, ALU.mult))
            f_ys.wait(pool, 1, j, apart=True)
            pool.indirect_dma_start(out, bass.IndirectOffsetOnAxis(tok_idx[:, par:par + 1], 0), ysb[par], None,
                                    compute_op=ALU.add).then_inc(s_add, 16)
            pool.wait_ge(s_add, r * 32 + 16 * (par + 1))
            pool.sem_inc(f_sa.sem, 1)
    sp.wait_ge(s_ld[0], 16 * (PAIRS + 2))
    sp.wait_ge(s_ld[1], 16 * (PAIRS + 2))
    sp.wait_ge(s_add, 16 * 2 * PAIRS)
    sp.wait_ge(s_out, 16 * (NB + 1))


_INS = ['x', 'src', 'dst', 'L0_gnn_W', 'L0_gnn_b', 'L0_ffn_gamma', 'L0_ffn_beta', 'L0_ffn_Wr', 'L0_ffn_br',
        'L0_ffn_W1', 'L0_ffn_b1', 'L0_ffn_W2', 'L0_ffn_b2']


def kernel(**inputs):
    import numpy as _np
    import concourse.bacc as _bacc
    from concourse import mybir as _mybir
    from concourse.bass_utils import run_bass_kernel_spmd as _run

    nc = _bacc.Bacc("TRN2", target_bir_lowering=False, num_devices=1)
    arrays, args = {}, []
    for name in _INS:
        a = _np.ascontiguousarray(inputs[name])
        arrays[f"in_{name}_dram"] = a
        args.append(nc.dram_tensor(f"in_{name}_dram", a.shape, _mybir.dt.from_np(a.dtype), kind="ExternalInput").ap())
    n, d = inputs['x'].shape
    rows = (-(-n // P) + 1) * P
    args.append(nc.dram_tensor("out_dram", (rows, d), _mybir.dt.float32, kind="ExternalOutput").ap())
    build(nc, *args)
    r = _run(nc, [arrays], core_ids=[0])
    return r.results[0]["out_dram"][:n]
```

```python
from contextlib import ExitStack

import concourse.bass as bass
from concourse import mybir

F32 = mybir.dt.float32
BF16 = mybir.dt.bfloat16
I32 = mybir.dt.int32
U32 = mybir.dt.uint32
ALU = mybir.AluOpType
ACT = mybir.ActivationFunctionType
AX_X = mybir.AxisListType.X
ds = bass.ds

P = 128
CREDIT = 16
EPS = 1e-5


class Event:

    def __init__(self, nc, name, per=1, credit_by=None):
        self.sem = nc.alloc_semaphore(name)
        self.per, self.done, self.credit = per, 0, 0
        if credit_by is not None:
            self.credit = per
            credit_by.sem_inc(self.sem, per)

    def inc(self, instruction):
        instruction.then_inc(self.sem, 1)
        self.done += 1
        return self.done

    def wait(self, engine, n=None, round=0, back=0, apart=False):
        n = self.per if n is None else n
        value = round * self.per + (n + self.credit - back * self.per)
        if apart and not isinstance(round, int):
            value = engine.to_reg(value)
            engine.wait_ge(self.sem, 1)
        engine.wait_ge(self.sem, value)


class Chain(Event):

    def begin(self, round=0):
        self.done, self.round = 0, round

    def then(self, engine, instruction, apart=False):
        n = self.inc(instruction)
        self.wait(engine, n, self.round, apart=apart)
        return n

    def end(self):
        assert self.done == self.per, (self.done, self.per)


def build(nc, x, src, dst, gnn_w, gnn_b, gamma, beta, wr, br, w1, b1, w2, b2, out):
    pe, dve, act, pool, sp = nc.tensor, nc.vector, nc.scalar, nc.gpsimd, nc.sync
    N, D = x.shape
    (E,) = src.shape
    X, _, H = w1.shape
    DO = w2.shape[2]
    DC = D // P
    HC = H // P
    NT = -(-N // P)
    ET = -(-E // P)
    TAIL = N - (NT - 1) * P
    B = 7
    NB = NT // B
    assert NT == B * NB and NB % 2 == 1 and D == 256 and DO == D and H == 512 and X == 8
    SPR = 17
    STEPS = SPR * NT
    assert STEPS >= ET + NT - 1
    HALF = 9
    SB = STEPS // B
    assert SB * B == STEPS and SB <= P
    TABLE = STEPS - NT + 1
    FIRSTS = ET - 1
    ROW = D + 4
    QUEUE = (NT + 1) * P
    IDLE = X * QUEUE
    TRASH = IDLE + P
    QROWS = TRASH + 2 * P
    QUEUE_TILES = (2 * N + X * (P - 1)) // P
    PAIRS = -(-QUEUE_TILES // 2)
    QT = 2 * PAIRS + 4
    OUT_ROWS = out.shape[0]
    assert OUT_ROWS >= N + P and OUT_ROWS >= NT * P

    def sb(name, shape, dt=F32):
        return nc.alloc_sbuf_tensor(name, shape, dt)

    g_rows = nc.dram_tensor("g_rows", (NT * P, D), F32).ap()
    src_tab = nc.dram_tensor("src_tab", (TABLE * P,), I32).ap()
    dst_tab = nc.dram_tensor("dst_tab", (TABLE * P,), I32).ap()
    b1_new = nc.dram_tensor("b1_new", (X, H), F32).ap()
    queue = nc.dram_tensor("queue", (QROWS, ROW), F32).ap()

    w1_sb = sb("w1_sb", [P, X, DC, H])
    region = sb("region", [P, X * HC * DO])
    xall = sb("xall", [P, NT, D])
    GW = D + 1
    acc = sb("acc", [P, NT * GW])
    acc3 = acc[:, :].rearrange("p (t c) -> p t c", t=NT)
    pay = sb("pay", [P, 2, B, ROW])
    pairbuf = sb("pairbuf", [P, 4, D])
    rowsb, trsb = pairbuf[:, 0:2, :], pairbuf[:, 2:4, :]
    wgt = sb("wgt", [P, 2 * DC, D])
    ident = sb("ident", [P, P])
    ones = sb("ones", [P, P])
    tri_b = sb("tri_b", [P, P], BF16)
    ones_b = sb("ones_b", [P, P], BF16)
    iota = sb("iota", [P, P])
    pcol = sb("pcol", [P, 1])
    pcol_i = sb("pcol_i", [P, 1], I32)
    gb_row = sb("gb_row", [1, D])
    n_row = sb("n_row", [1, STEPS], I32)
    mv = sb("mv", [P, B, 2])
    rstd = sb("rstd", [P, NT])
    nmr = sb("nmr", [P, NT])
    beta_at = sb("beta_at", [P, DC, X * X])
    b1_sb = sb("b1_sb", [X, H])
    stats = sb("stats", [P, B, 6])
    sd = sb("sd", [P, B])
    idx_a = sb("idx_a", [P, HALF], I32)
    idx_b = sb("idx_b", [P, SPR - HALF], I32)
    wr_sb = sb("wr_sb", [P, DC, X])
    br_row = sb("br_row", [1, X])
    gam = sb("gam", [P, DC])
    bet = sb("bet", [P, DC])

    def at(base, offset, *shape):
        n = 1
        for s in shape:
            n *= s
        v = base[:, offset:offset + n]
        if len(shape) == 2:
            v = v.rearrange("p (a b) -> p a b", a=shape[0])
        return v, offset + n

    pay_flat = pay[:, :, :, :].rearrange("p a b c -> p (a b c)")
    fst_i, o = at(region, 0, FIRSTS)
    fst_f, o = at(region, o, FIRSTS)
    below, o = at(region, o, FIRSTS)
    passed, o = at(region, o, STEPS)
    tab_i, o = at(region, o, 2 * B, P)
    tab_f, o = at(region, o, 2 * B, P)
    fst_i, tab_i = fst_i.bitcast(I32), tab_i.bitcast(I32)
    RELW = STEPS + SPR
    assert o <= X * HC * DO - RELW
    rel, _ = at(region, X * HC * DO - RELW, RELW)
    grow, o = at(region, 0, SPR, GW)
    hot_a, o = at(region, o, HALF, P)
    hot_b, o = at(region, o, SPR - HALF, P)
    assert o <= X * HC * DO - RELW
    w2_sb = region[:, :].rearrange("p (e k o) -> p e k o", e=X, k=HC)
    iota_i, o = at(pay_flat, 0, STEPS)
    iota_f, o = at(pay_flat, o, STEPS)
    srcs, o = at(pay_flat, o, RELW)
    iota_i, srcs = iota_i.bitcast(I32), srcs.bitcast(I32)
    wg_sb, o = at(pay_flat, o, 2, 2 * D)
    assert o <= 2 * B * ROW
    pad_i = pairbuf[:, 0:4, :].rearrange("p a b -> p (a b)")[0:1, 0:8 * P].rearrange("p (a b) -> p a b", a=2).bitcast(I32)
    w1_flat = w1_sb[:, :, :, :].rearrange("p e c h -> p (e c h)")
    stage = [at(w1_flat, k * B * D, B, D)[0] for k in range(2)]
    LATE = -(-2 * B * D // (DC * H))

    psum = [nc.alloc_psum_tensor(f"psum{n}", [P, 512], F32) for n in range(8)]

    def sem(name):
        return nc.alloc_semaphore(name)

    c_dve = Chain(nc, "c_dve")
    c_dve.begin()
    c_dve.per = 0
    c_pool = Chain(nc, "c_pool")
    c_pool.begin()
    c_pool.per = 0
    c_pe = Chain(nc, "c_pe")
    c_pe.begin()
    c_pe.per = 0

    s_edges, s_fst, s_small, s_gw, s_w1 = (sem(n) for n in ("s_edges", "s_fst", "s_small", "s_gw", "s_w1"))
    act.dma_start(src_tab[0:E], src[:]).then_inc(s_edges, 16)
    act.dma_start(dst_tab[0:E], dst[:]).then_inc(s_edges, 16)
    act.dma_start(fst_i[0:1, :], dst[P:E:P].unsqueeze(0), allow_slow_non_contiguous=True).then_inc(s_fst, 16)
    act.dma_start(wg_sb[:, :, :], gnn_w.rearrange("(o p) i -> p o i", p=P)).then_inc(s_gw, 16)
    act.dma_start(gb_row[:, :], gnn_b.unsqueeze(0)).then_inc(s_small, 16)
    act.dma_start(gam[:, :], gamma.rearrange("(c p) -> p c", p=P), allow_slow_non_contiguous=True).then_inc(s_small, 16)
    act.dma_start(bet[:, :], beta.rearrange("(c p) -> p c", p=P), allow_slow_non_contiguous=True).then_inc(s_small, 16)
    act.dma_start(wr_sb[:, :, :], wr.rearrange("(c p) e -> p c e", p=P)).then_inc(s_small, 16)
    act.dma_start(br_row[:, :], br.unsqueeze(0)).then_inc(s_small, 16)
    act.dma_start(b1_sb[:, :], b1).then_inc(s_small, 16)

    pool.iota(iota_i, [[1, STEPS]], channel_multiplier=0)
    t_iota = c_pool.inc(pool.iota(pcol_i[:, :], [[0, 1]], channel_multiplier=1))
    step_i = sb("step_i", [P, B], I32)
    t_step = c_pool.inc(pool.iota(step_i[:, :], [[SB, B]], channel_multiplier=1))
    t_zeros = c_pool.inc(pool.memset(acc[:, :], 0.0))
    PADN = TABLE * P - E
    dve.memset(pad_i[:, 0, :], 0)
    t_pad = c_dve.inc(dve.memset(pad_i[:, 1, :], 2 * NT * P))
    c_dve.wait(sp, t_pad)
    sp.dma_start(src_tab[E:E + PADN].unsqueeze(0), pad_i[:, 0, 0:PADN]).then_inc(s_edges, 16)
    sp.dma_start(dst_tab[E:E + PADN].unsqueeze(0), pad_i[:, 1, 0:PADN]).then_inc(s_edges, 16)
    t_tail = c_dve.inc(dve.memset(xall[96:P, NT - 1, :], 0.0))
    dve.memset(ones[:, :], 1.0)
    dve.memset(ones_b[:, :], 1.0)
    c_pool.wait(dve, t_iota)
    dve.tensor_copy(iota[:, :], iota_i[:, 0:P])
    dve.tensor_copy(iota_f, iota_i)
    c_dve.then(dve, dve.tensor_copy(pcol[:, :], pcol_i[:, :]))
    dve.tensor_scalar(ident[:, :], iota[:, :], pcol[:, 0:1], None, ALU.is_equal)
    bound = sb("bound", [P, 1])
    dve.tensor_scalar(bound[:, :], pcol[:, :], float(P), float(P), ALU.mult, ALU.add)
    t_const = c_dve.inc(dve.tensor_scalar(tri_b[:, :], iota[:, :], pcol[:, 0:1], None, ALU.is_gt))

    s_x, s_tail = [sem("s_x0"), sem("s_x1")], sem("s_tail")
    for b in range(NB):
        if b == 1:
            c_dve.wait(sp, t_tail)
            sp.dma_start(xall[0:TAIL, NT - 1, :], x[(NT - 1) * P:N, :]).then_inc(s_tail, 16)
        if b >= 2:
            sp.wait_ge(s_x[b % 2], 16 * (b // 2))
        t0, t1 = b * B, min((b + 1) * B, NT - 1)
        sp.dma_start(xall[:, t0:t1, :], x[t0 * P:t1 * P, :].rearrange("(t p) d -> p t d", p=P)).then_inc(s_x[b % 2], 16)
    for e in range(LATE, X):
        sp.dma_start(w1_sb[:, e, :, :], w1[e].rearrange("(c p) h -> p c h", p=P)).then_inc(s_w1, 16)

    c_dve.wait(pe, t_const)
    pe.wait_ge(s_gw, 16)
    for c in range(2 * DC):
        for o_ in range(2):
            i = pe.transpose(psum[4 + c // 2][:, (c % 2) * D + o_ * P:(c % 2) * D + (o_ + 1) * P],
                             wg_sb[:, o_, c * P:(c + 1) * P], ident[:, :])
    t = c_pe.inc(i)
    c_pe.wait(dve, t)
    for g in range(DC):
        i = dve.tensor_copy(wgt[:, 2 * g:2 * g + 2, :].rearrange("p a b -> p (a b)"), psum[4 + g][:, :])
    t_wgt = c_dve.inc(i)

    ln = Chain(nc, "ln_dve", per=5)
    ln_sd = Event(nc, "ln_sd")

    def tile_stats(b, j):
        return dve.bn_stats(stats[:, j, :], xall[:, ds(b * B + j, 1), :].rearrange("p a d -> p (a d)"))

    def scales(b, stats_done):
        ln.begin(b)
        ln.then(dve, stats_done, apart=True)
        for j in range(B):
            i = dve.bn_aggr(mv[:, j, :], stats[:, j, :])
        ln.then(dve, i)
        t = ln.inc(dve.tensor_scalar(sd[:, :], mv[:, :, 1], EPS, None, ALU.add))
        ln.wait(act, t, b)
        ln_sd.inc(act.activation(sd[:, :], sd[:, :], ACT.Sqrt))
        ln_sd.wait(dve, 1, b)
        r = rstd[:, ds(b * B, B)]
        ln.then(dve, dve.reciprocal(r, sd[:, :]))
        ln.inc(dve.scalar_tensor_tensor(nmr[:, ds(b * B, B)], mv[:, :, 0], -1.0, r, ALU.mult, ALU.mult))
        ln.end()

    dve.wait_ge(s_fst, 16)
    t_fst = c_dve.inc(dve.tensor_copy(fst_f[0:1, :], fst_i[0:1, :]))
    c_dve.wait(pe, t_fst)
    pe.matmul(psum[0][0:NT, 0:512], ones[0:1, 0:NT], fst_f[0:1, 0:512], start=True, stop=True)
    t = c_pe.inc(pe.matmul(psum[1][0:NT, 0:FIRSTS - 512], ones[0:1, 0:NT], fst_f[0:1, 512:FIRSTS], start=True, stop=True))
    c_pe.wait(dve, t)
    c_dve.wait(dve, t_const)
    dve.tensor_scalar(below[0:NT, 0:512], psum[0][0:NT, 0:512], bound[0:NT, 0:1], None, ALU.is_lt)
    c_dve.then(dve, dve.tensor_scalar(below[0:NT, 512:FIRSTS], psum[1][0:NT, 0:FIRSTS - 512], bound[0:NT, 0:1], None, ALU.is_lt))
    key = sb("key", [P, 1])
    c_dve.then(dve, dve.tensor_reduce(key[0:NT, :], below[0:NT, :], AX_X, ALU.add))
    c_dve.then(dve, dve.tensor_tensor(key[0:NT, :], key[0:NT, :], pcol[0:NT, :], ALU.add))
    t = c_dve.inc(dve.tensor_scalar(passed[0:NT, :], iota_f[0:NT, :], key[0:NT, 0:1], None, ALU.is_gt))
    dve.wait_ge(s_tail, 16)
    dve.wait_ge(s_x[0], 16)
    for j in range(B):
        i = tile_stats(0, j)
    scales(0, i)
    c_dve.wait(pe, t)
    pe.matmul(psum[0][0:1, 0:512], ones[0:NT, 0:1], passed[0:NT, 0:512], start=True, stop=True)
    pe.matmul(psum[1][0:1, 0:STEPS - 512], ones[0:NT, 0:1], passed[0:NT, 512:STEPS], start=True, stop=True)
    for b in range(B):
        m = pe.matmul(psum[2][0:SB, b:b + 1], passed[0:NT, b * SB:(b + 1) * SB], ones[0:NT, 0:1], start=True, stop=True)
    t = c_pe.inc(m)
    c_pe.wait(dve, t)
    last = float(NT - 1)
    dve.tensor_scalar(n_row[0:1, 0:512], psum[0][0:1, 0:512], last, None, ALU.min)
    t_nrow = c_dve.inc(dve.tensor_scalar(n_row[0:1, 512:STEPS], psum[1][0:1, 0:STEPS - 512], last, None, ALU.min))
    n_col, step_col, e_col, e_idx = sb("n_col", [P, B]), sb("step_col", [P, B]), sb("e_col", [P, B]), sb("e_idx", [P, B], I32)
    c_pool.wait(dve, t_step)
    dve.tensor_copy(step_col[:, :], step_i[:, :])
    c_dve.then(dve, dve.tensor_scalar(n_col[0:SB, :], psum[2][0:SB, 0:B], last, None, ALU.min))
    c_dve.then(dve, dve.tensor_tensor(e_col[0:SB, :], step_col[0:SB, :], n_col[0:SB, :], ALU.subtract))
    t = c_dve.inc(dve.tensor_copy(e_idx[0:SB, :], e_col[0:SB, :]))
    t_ncol = c_dve.inc(dve.tensor_scalar(n_col[0:SB, :], n_col[0:SB, :], float(P), None, ALU.mult))
    c_dve.wait(pool, t)
    pool.wait_ge(s_edges, 64)
    s_tab = sem("s_tab")
    for k, tab in enumerate((src_tab, dst_tab)):
        tiles = tab.rearrange("(a b) -> a b", b=P)
        for b in range(B):
            pool.indirect_dma_start(tab_i[0:SB, k * B + b, :], None, tiles,
                                    bass.IndirectOffsetOnAxis(e_idx[0:SB, b:b + 1], 0)).then_inc(s_tab, 16)

    pool.wait_ge(s_tab, 16 * 2 * B)
    c_dve.wait(pool, t_ncol)
    c_pool.then(pool, pool.tensor_copy(tab_f[0:SB, :, :], tab_i[0:SB, :, :]))
    t_tabf = c_pool.inc(pool.tensor_tensor(tab_f[0:SB, B:2 * B, :], tab_f[0:SB, B:2 * B, :],
                                           n_col[0:SB, :].unsqueeze(2).broadcast_to([SB, B, P]), ALU.subtract))

    s_g = [sem("s_g0"), sem("s_g1")]
    n_h = Event(nc, "n_h", 2 * B)
    n_tr = Event(nc, "n_tr", 2 * B)
    n_cp = Event(nc, "n_cp", 2 * B)
    n_mm = Event(nc, "n_mm", 2 * B)
    n_g = Event(nc, "n_g", 2 * B)
    for ev, eng in ((n_cp, dve), (n_mm, pe), (n_g, act)):
        ev.credit = 2
        eng.sem_inc(ev.sem, 2)
    for k in range(2):
        act.sem_inc(s_g[k], CREDIT)

    def tile_h(r, s, t):
        if t >= 2:
            n_tr.wait(act, s - 1, r)
        n_h.inc(act.activation(rowsb[:, s % 2, :], xall[:, ds(r * (2 * B) + s, 1), :].rearrange("p a d -> p (a d)"), ACT.Identity,
                               bias=nmr[:, ds(r * (2 * B) + s, 1)], scale=rstd[:, ds(r * (2 * B) + s, 1)]))

    def tile_transpose(r, s):
        n_h.wait(pe, s + 1, r)
        n_cp.wait(pe, s - 1, r)
        for c in range(DC):
            i = pe.transpose(psum[s % 2][:, c * P:(c + 1) * P], rowsb[:, s % 2, c * P:(c + 1) * P], ident[:, :])
        n_tr.inc(i)
        n_tr.wait(dve, s + 1, r)
        n_mm.wait(dve, s - 1, r)
        n_cp.inc(dve.tensor_copy(trsb[:, s % 2, :], psum[s % 2][:, 0:D]))

    def tile_product(r, s):
        n_cp.wait(pe, s + 1, r)
        n_g.wait(pe, s - 1, r)
        for c in range(DC):
            i = pe.matmul(psum[2 + s % 2][:, 0:D], trsb[:, s % 2, c * P:(c + 1) * P], wgt[:, DC + c, :],
                          start=(c == 0), stop=(c == DC - 1))
        n_mm.inc(i)

    def norm(r, half, last=False):
        b = r * 2 + half
        for j in range(B):
            s = half * B + j
            if not last or j + 2 < B:
                tile_h(r, s + 2, 2)
            if not last or j + 1 < B:
                tile_transpose(r, s + 1)
            tile_product(r, s)
            if not last:
                if j == 0:
                    dve.wait_ge(s_x[1 - half], r * 16 + 16 * (half + 1))
                for q in range(3 * j, min(3 * j + 3, B)):
                    last_stats = tile_stats(b + 1, q)
                if j == 3:
                    scales(b + 1, last_stats)
                if j == B - 3:
                    ln.wait(act, None, b + 1)
            if j == 0:
                act.wait_ge(s_g[half], r * 16 + CREDIT)
            n_mm.wait(act, s + 1, r)
            n_g.inc(act.copy(stage[half][:, j, :], psum[2 + s % 2][:, 0:D]))
        n_g.wait(act, s + 1, r)
        act.dma_start(g_rows[ds(b * (B * P), B * P), :].rearrange("(t p) d -> p t d", p=P), stage[half]).then_inc(s_g[half], 16)

    c_dve.wait(pe, t_wgt)
    dve.wait_ge(s_edges, 64)
    act.wait_ge(s_edges, 64)
    ln.wait(act, None, 0)
    tile_h(0, 0, 0)
    tile_h(0, 1, 1)
    tile_transpose(0, 0)
    with nc.Fori(0, NB // 2) as r:
        norm(r, 0)
        norm(r, 1)

    c_pool.wait(pe, t_tabf)
    groups = [(0, 4), (4, B)]
    for k in range(2):
        for g, (lo, hi) in enumerate(groups):
            for b in range(lo, hi):
                i = pe.transpose(psum[4 + 2 * k + g][:, (b - lo) * SB:(b - lo + 1) * SB], tab_f[0:SB, k * B + b, :], ident[0:SB, 0:SB])
    t = c_pe.inc(i)
    norm(NB // 2, 0, last=True)
    c_pe.wait(dve, t)
    dve.memset(rel[:, STEPS:RELW], -1.0)
    dve.memset(srcs[:, STEPS:RELW], 0)
    for g, (lo, hi) in enumerate(groups):
        dve.tensor_copy(srcs[:, lo * SB:hi * SB], psum[4 + g][:, 0:(hi - lo) * SB])
        i = dve.tensor_copy(rel[:, lo * SB:hi * SB], psum[6 + g][:, 0:(hi - lo) * SB])
    t_rel = c_dve.inc(i)

    step_mm = Event(nc, "step_mm", SPR, credit_by=pe)
    step_add = Event(nc, "step_add", SPR, credit_by=dve)
    hot_a_up = Event(nc, "hot_a_up")
    hot_b_up = Event(nc, "hot_b_up")
    idx_a_up = Event(nc, "idx_a_up")
    idx_b_up = Event(nc, "idx_b_up")
    own_h = Event(nc, "own_h")
    own_tr = Event(nc, "own_tr")
    own_cp = Event(nc, "own_cp")
    own_mm = Event(nc, "own_mm")
    own_add = Event(nc, "own_add", credit_by=dve)
    got = [sem(f"got{k}") for k in range(SPR)]
    BANKS = 4

    def one_hot(out_t, first, n):
        return dve.tensor_tensor(out_t, iota[:, :].unsqueeze(1).broadcast_to([P, n, P]),
                                 rel[:, ds(first, n)].unsqueeze(2).broadcast_to([P, n, P]), ALU.is_equal)

    c_dve.wait(dve, t_rel)
    t_ones = c_dve.inc(dve.memset(grow[:, :, D:GW], 1.0))
    hot_a_up.inc(one_hot(hot_a, 0, HALF))
    c_pool.wait(dve, t_zeros)
    c_dve.wait(dve, t_nrow)
    c_dve.wait(act, t_rel)
    idx_a_up.inc(act.copy(idx_a[:, :], srcs[:, 0:HALF]))
    idx_b_up.inc(act.copy(idx_b[:, :], srcs[:, HALF:SPR]))
    c_dve.wait(pe, t_ones)
    c_dve.wait(pool, t_rel)
    pool.wait_ge(s_g[0], 16 * (NB // 2 + 1) + CREDIT)
    pool.wait_ge(s_g[1], 16 * (NB // 2) + CREDIT)

    sp.wait_ge(s_g[0], 16 * (NB // 2 + 1) + CREDIT)
    sp.wait_ge(s_g[1], 16 * (NB // 2) + CREDIT)
    s_w1_late = sem("s_w1_late")
    for e in range(LATE):
        sp.dma_start(w1_sb[:, e, :, :], w1[e].rearrange("(c p) h -> p c h", p=P)).then_inc(s_w1_late, 16)

    pe.wait_ge(s_w1, 16 * (X - LATE))
    pe.wait_ge(s_small, 16 * 6)
    dve.wait_ge(s_small, 16 * 6)
    c_dve.then(dve, dve.memset(beta_at[:, :, :], 0.0))
    for c in range(DC):
        i = dve.tensor_copy(beta_at[:, c, 0:X * X:X + 1], bet[:, c:c + 1].broadcast_to([P, X]))
    t = c_dve.inc(i)
    c_dve.wait(pe, t)
    for c in range(DC):
        pe.matmul(psum[6][0:1, 0:X], bet[:, c:c + 1], wr_sb[:, c, :], start=(c == 0), stop=False)
    pe.matmul(psum[6][0:1, 0:X], ones[0:1, 0:1], br_row[0:1, :], start=False, stop=True)
    for e in [*range(LATE, X), *range(LATE)]:
        if e == 0:
            pe.wait_ge(s_w1_late, 16 * LATE)
        for c in range(DC):
            i = pe.matmul(psum[7][0:X, :], beta_at[:, c, e * X:(e + 1) * X], w1_sb[:, e, c, :],
                          start=(e == LATE and c == 0), stop=(e == LATE - 1 and c == DC - 1))
    t = c_pe.inc(i)
    c_pe.wait(dve, t)
    dve.tensor_copy(br_row[0:1, :], psum[6][0:1, 0:X])
    for c in range(DC):
        dve.tensor_scalar(wr_sb[:, c, :], wr_sb[:, c, :], gam[:, c:c + 1], None, ALU.mult)
    t_b1 = c_dve.inc(dve.tensor_tensor(b1_sb[:, :], b1_sb[:, :], psum[7][0:X, :], ALU.add))
    s_b1 = sem("s_b1")
    c_dve.wait(sp, t_b1)
    sp.dma_start(b1_new, b1_sb[:, :]).then_inc(s_b1, 16)

    window_of = [dve.alloc_register(f"window{k}") for k in range(SPR)]
    with nc.Fori(0, NT) as r:
        first = r * SPR
        hot_a_free, hot_b_free = HALF, SPR
        dve.load(window_of, n_row[0:1, ds(first, SPR)])
        step_mm.wait(dve, hot_b_free, r, back=1)
        hot_b_up.inc(one_hot(hot_b, first + HALF, SPR - HALF))
        own_h.inc(act.activation(rowsb[:, 0, :], xall[:, ds(r, 1), :].rearrange("p a d -> p (a d)"), ACT.Identity,
                                 bias=nmr[:, ds(r, 1)], scale=rstd[:, ds(r, 1)]))
        for k in range(SPR):
            if k in (0, HALF):
                (idx_a_up if k < HALF else idx_b_up).wait(pool, 1, r)
            step_mm.wait(pool, k + 1, r, back=1, apart=True)
            idx = idx_a[:, k:k + 1] if k < HALF else idx_b[:, k - HALF:k - HALF + 1]
            pool.indirect_dma_start(grow[:, k, 0:D], None, g_rows, bass.IndirectOffsetOnAxis(idx, 0)).then_inc(got[k], 16)
            bank = psum[k % BANKS]
            pe.wait_ge(got[k], r * 16 + 16)
            if k == 0:
                hot_a_up.wait(pe, 1, r)
            if k == HALF:
                hot_b_up.wait(pe, 1, r)
            if k >= BANKS:
                step_add.wait(pe, k - BANKS + 1, r)
            else:
                step_add.wait(pe, max(q for q in range(SPR) if q % BANKS == k) + 1, r, back=1)
            hot = hot_a[:, k, :] if k < HALF else hot_b[:, k - HALF, :]
            step_mm.inc(pe.matmul(bank[:, 0:GW], hot, grow[:, k, :], start=True, stop=True))
            window = dve.snap(window_of[k], donate=True, min_val=0, max_val=NT - 1)
            sums = acc3[:, ds(window, 1), :].rearrange("p a c -> p (a c)")
            step_mm.wait(dve, k + 1, r)
            if k:
                step_add.wait(dve, k, r)
            else:
                step_add.wait(dve, SPR, r, back=1)
            step_add.inc(dve.tensor_tensor(sums, sums, bank[:, 0:GW], ALU.add))
            if k == 2:
                own_h.wait(pe, 1, r)
                for c in range(DC):
                    i = pe.transpose(psum[4][:, c * P:(c + 1) * P], rowsb[:, 0, c * P:(c + 1) * P], ident[:, :])
                own_tr.inc(i)
                own_tr.wait(act, 1, r)
                own_cp.inc(act.copy(trsb[:, 0, :], psum[4][:, 0:D]))
            if k == 6:
                own_cp.wait(pe, 1, r)
                own_add.wait(pe, 1, r, back=1)
                for c in range(DC):
                    pe.matmul(psum[5][:, 0:D], trsb[:, 0, c * P:(c + 1) * P], wgt[:, c, :], start=(c == 0), stop=False)
                own_mm.inc(pe.matmul(psum[5][:, 0:D], ones[0:1, :], gb_row[0:1, :], start=False, stop=True))
            if k == HALF - 1:
                step_mm.wait(dve, HALF, r)
                hot_a_up.inc(one_hot(hot_a, first + SPR, HALF))
                step_mm.wait(act, HALF, r)
                idx_a_up.inc(act.copy(idx_a[:, :], srcs[:, ds(first + SPR, HALF)]))
            if k == HALF:
                own_mm.wait(dve, 1, r)
                xt = xall[:, ds(r, 1), :].rearrange("p a d -> p (a d)")
                own_add.inc(dve.tensor_tensor(xt, xt, psum[5][:, 0:D], ALU.add))
        step_mm.wait(act, SPR, r)
        idx_b_up.inc(act.copy(idx_b[:, :], srcs[:, ds(first + SPR + HALF, SPR - HALF)]))

    s_w2 = sem("s_w2")
    step_mm.wait(sp, SPR, NT - 1)
    step_add.wait(sp, SPR, NT - 1)
    hot_a_up.wait(sp, 1, NT)
    for e in range(X):
        sp.dma_start(w2_sb[:, e, :, :], w2[e].rearrange("(k p) o -> p k o", p=P)).then_inc(s_w2, 16)

    rdeg = sb("rdeg", [P, NT])
    valid = sb("valid", [P, NT])
    tok = sb("tok", [P, NT])
    trash = sb("trash", [P, 2, NT])
    tok_i = sb("tok_i", [P, NT], I32)
    carry = sb("carry", [P, X])
    qbase = sb("qbase", [P, X])
    qbase_i = sb("qbase_i", [P, X], I32)
    s_out = sem("s_out")
    c_pool2 = Chain(nc, "c_pool2")
    c_pool2.begin()
    pool.iota(tok_i[:, :], [[P, NT]], channel_multiplier=1)
    t = c_pool2.inc(pool.iota(qbase_i[:, :], [[QUEUE, X]], channel_multiplier=0))
    c_pool2.wait(dve, t)
    c2 = Chain(nc, "c2")
    c2.begin()
    step_add.wait(dve, SPR, NT - 1)
    dve.tensor_copy(tok[:, :], tok_i[:, :])
    dve.tensor_copy(qbase[:, :], qbase_i[:, :])
    c2.then(dve, dve.tensor_scalar(rdeg[:, :], acc3[:, :, D:GW].rearrange("p a o -> p (a o)"), 1.0, None, ALU.max))
    c2.then(dve, dve.reciprocal(rdeg[:, :], rdeg[:, :]))
    dve.tensor_copy(carry[:, :], qbase[:, :])
    c2.then(dve, dve.tensor_scalar(valid[:, :], tok[:, :], float(N), None, ALU.is_lt))
    c2.then(dve, dve.tensor_scalar(trash[:, 1, :], valid[:, :], -1.0, 1.0, ALU.mult, ALU.add))
    c2.then(dve, dve.tensor_scalar(bound[:, :], pcol[:, :], float(TRASH), None, ALU.add))
    c2.then(dve, dve.tensor_scalar(trash[:, 0, :], trash[:, 1, :], bound[:, 0:1], None, ALU.mult))
    t_rt = c2.then(dve, dve.scalar_tensor_tensor(trash[:, 1, :], trash[:, 1, :], float(P), trash[:, 0, :], ALU.mult, ALU.add))
    zero = sb("zero", [P, D])
    t_zero = c2.inc(dve.memset(zero[:, :], 0.0))
    c2.wait(sp, t_zero)
    sp.dma_start(out[NT * P:NT * P + P, :], zero[:, :]).then_inc(s_out, 16)
    c2.wait(act, t_rt)

    small = sb("small", [P, 8, B])
    u1, sd2, rr, nm, dif, ex, wa, wb = (small[:, n, :] for n in range(8))
    lg = sb("lg", [P, B, X])
    top = sb("top", [P, B, X])
    topi = sb("topi", [P, B, X], U32)
    e12 = sb("e12", [P, B, 2])
    pick = sb("pick", [P, 2, B, X])
    both = sb("both", [P, B, X], BF16)
    both_f = sb("both_f", [P, B, X])
    rank = sb("rank", [P, B, X])
    prod = sb("prod", [P, 2, B, X])
    slot = sb("slot", [P, 2, B])
    BUFS = 3
    assert NB % BUFS == 1
    slot_i = sb("slot_i", [P, BUFS, 2, B], I32)
    total = sb("total", [P, X])
    payload = [pay[:, 0, :, :], pay[:, 1, :, :], at(acc, 0, B, ROW)[0]]
    assert B * ROW <= 2 * B * GW

    g_st = Chain(nc, "g_st", per=7)
    g_sq = Event(nc, "g_sq")
    g_xh = Event(nc, "g_xh", credit_by=act)
    g_tx = Event(nc, "g_tx", B)
    g_xt = Event(nc, "g_xt", B)
    g_lg = Event(nc, "g_lg", B)
    g_ex = Event(nc, "g_ex")
    g_rk = Event(nc, "g_rk")
    s_sc = [sem(f"s_sc{k}") for k in range(BUFS)]
    g_sent = Event(nc, "g_sent")
    SCATTERS = 16 * 2 * B
    ch = Chain(nc, "router_dve", per=18)

    def features(b, buf):
        g_st.begin(b)
        tile = lambda v, j: v[:, ds(b * B + j, 1), :].rearrange("p a d -> p (a d)")
        for j in range(B):
            i = dve.scalar_tensor_tensor(tile(xall, j), acc3[:, ds(b * B + j, 1), 0:D].rearrange("p a d -> p (a d)"),
                                         rdeg[:, ds(b * B + j, 1)], tile(xall, j), ALU.mult, ALU.add)
        t = g_st.then(dve, i, apart=True)
        g_st.wait(sp, t, b)
        sp.dma_start(out[ds(b * (B * P), B * P), :].rearrange("(t p) d -> p t d", p=P), xall[:, ds(b * B, B), :]).then_inc(s_out, 16)
        for j in range(B):
            i = dve.bn_stats(stats[:, j, :], tile(xall, j))
        g_st.then(dve, i, apart=True)
        for j in range(B):
            i = dve.bn_aggr(mv[:, j, :], stats[:, j, :])
        g_st.then(dve, i)
        mean, var = mv[:, :, 0], mv[:, :, 1]
        g_st.then(dve, dve.tensor_scalar(u1, var, EPS, EPS, ALU.add, ALU.mult))
        t = g_st.inc(dve.tensor_tensor(u1, u1, var, ALU.add))
        g_st.wait(act, t, b)
        g_sq.inc(act.activation(sd2, u1, ACT.Sqrt))
        g_xh.wait(dve, 1, b, back=1)
        g_sq.wait(dve, 1, b)
        g_st.then(dve, dve.reciprocal(rr, sd2))
        t = g_st.inc(dve.scalar_tensor_tensor(nm, mean, -1.0, rr, ALU.mult, ALU.mult))
        g_st.end()
        g_st.wait(act, t, b)
        g_sent.wait(act, 1, b, back=BUFS)
        for j in range(B):
            i = act.activation(payload[buf][:, j, 0:D], tile(xall, j), ACT.Identity, bias=nm[:, j:j + 1], scale=rr[:, j:j + 1])
        g_xh.inc(i)

    def logits(b, buf):
        g_xh.wait(pe, 1, b)
        for j in range(B + 1):
            if j < B:
                if j >= 2:
                    g_xt.wait(pe, j - 1, b)
                for c in range(DC):
                    i = pe.transpose(psum[j % 2][:, c * P:(c + 1) * P], payload[buf][:, j, c * P:(c + 1) * P], ident[:, :])
                g_tx.inc(i)
                g_tx.wait(act, j + 1, b)
                if j >= 2:
                    g_lg.wait(act, j - 1, b)
                g_xt.inc(act.copy(trsb[:, j % 2, :], psum[j % 2][:, 0:D]))
            if j >= 1:
                q = j - 1
                g_xt.wait(pe, q + 1, b)
                cols = psum[4][:, q * X:(q + 1) * X]
                for c in range(DC):
                    pe.matmul(cols, trsb[:, q % 2, c * P:(c + 1) * P], wr_sb[:, c, :], start=(c == 0), stop=False)
                g_lg.inc(pe.matmul(cols, ones[0:1, :], br_row[0:1, :], start=False, stop=True))

    def route(b, buf):
        ch.begin(b)
        g_lg.wait(dve, B, b)
        ch.then(dve, dve.tensor_copy(lg[:, :, :].rearrange("p a b -> p (a b)"), psum[4][:, 0:B * X]), apart=True)
        for j in range(B):
            i = dve.max(top[:, j, :], lg[:, j, :])
        ch.then(dve, i, apart=True)
        t = ch.inc(dve.tensor_tensor(dif, top[:, :, 1], top[:, :, 0], ALU.subtract))
        ch.wait(act, t, b)
        g_ex.inc(act.activation(ex, dif, ACT.Exp))
        for j in range(B):
            i = dve.max_index(topi[:, j, :], top[:, j, :], lg[:, j, :])
        ch.then(dve, i)
        ch.then(dve, dve.tensor_copy(e12[:, :, :], topi[:, :, 0:2]))
        for s in range(2):
            i = dve.tensor_tensor(pick[:, s, :, :], iota[:, 0:X].unsqueeze(1).broadcast_to([P, B, X]),
                                  e12[:, :, s:s + 1].broadcast_to([P, B, X]), ALU.is_equal)
        ch.then(dve, i)
        ch.then(dve, dve.tensor_tensor(both_f[:, :, :], pick[:, 0, :, :], pick[:, 1, :, :], ALU.add))
        vb = valid[:, ds(b * B, B)]
        t = ch.inc(dve.tensor_tensor(both[:, :, :], both_f[:, :, :], vb.unsqueeze(2).broadcast_to([P, B, X]), ALU.mult))
        ch.wait(pe, t, b)
        rk = psum[5][:, 0:B * X].rearrange("p (a b) -> p a b", a=B)
        pe.matmul(rk, tri_b[:, :], both[:, :, :], start=True, stop=True)
        for j in range(B - 1):
            pe.matmul(rk[:, j + 1:B, :], ones_b[:, :], both[:, j:j + 1, :].broadcast_to([P, B - 1 - j, X]),
                      start=False, stop=True, skip_group_check=True)
        g_rk.inc(pe.matmul(psum[6][:, 0:B * X].rearrange("p (a b) -> p a b", a=B), ones_b[:, :], both[:, :, :], start=True, stop=True))
        g_ex.wait(dve, 1, b)
        ch.then(dve, dve.tensor_scalar(wa, ex, 1.0, None, ALU.add))
        ch.then(dve, dve.reciprocal(wa, wa))
        ch.then(dve, dve.tensor_tensor(wb, ex, wa, ALU.mult), apart=True)
        rows = payload[buf]
        dve.tensor_copy(rows[:, :, D:D + 1], tok[:, ds(b * B, B)].unsqueeze(2))
        dve.tensor_copy(rows[:, :, D + 1:D + 2], e12[:, :, 0:1])
        dve.tensor_tensor(rows[:, :, D + 2:D + 3], wa.unsqueeze(2), wb.unsqueeze(2), ALU.subtract)
        dve.tensor_copy(rows[:, :, D + 3:D + 4], wb.unsqueeze(2))
        g_rk.wait(dve, 1, b)
        ch.then(dve, dve.tensor_tensor(rank[:, :, :], rk, carry[:, :].unsqueeze(1).broadcast_to([P, B, X]), ALU.add))
        for s in range(2):
            i = dve.tensor_tensor(prod[:, s, :, :], rank[:, :, :], pick[:, s, :, :], ALU.mult)
        ch.then(dve, i)
        ch.then(dve, dve.tensor_reduce(slot[:, :, :], prod[:, :, :, :], AX_X, ALU.add))
        ch.then(dve, dve.tensor_tensor(slot[:, :, :], slot[:, :, :], vb.unsqueeze(1).broadcast_to([P, 2, B]), ALU.mult))
        t = ch.inc(dve.tensor_tensor(slot_i[:, buf, :, :], slot[:, :, :], trash[:, :, ds(b * B, B)], ALU.add))
        ch.wait(pool, t, b)
        g_xh.wait(pool, 1, b, apart=True)
        for j in range(B):
            for s in range(2):
                pool.indirect_dma_start(queue, bass.IndirectOffsetOnAxis(slot_i[:, buf, s, j:j + 1], 0),
                                        payload[buf][:, j, :], None).then_inc(s_sc[buf], 16)
        ch.then(dve, dve.tensor_reduce(total[:, :], psum[6][:, 0:B * X].rearrange("p (a b) -> p b a", a=B), AX_X, ALU.add))
        ch.then(dve, dve.tensor_tensor(carry[:, :], carry[:, :], total[:, :], ALU.add))
        ch.end()

    c_dve.wait(pe, t_b1)
    g_sent.credit = BUFS
    sp.sem_inc(g_sent.sem, BUFS)
    features(0, 0)
    with nc.Fori(0, NB // BUFS) as r:
        for k in range(BUFS):
            b = r * BUFS + k
            logits(b, k)
            features(b + 1, (k + 1) % BUFS)
            route(b, k)
            sp.wait_ge(s_sc[k], r * SCATTERS + SCATTERS)
            sp.sem_inc(g_sent.sem, 1)
    logits(NB - 1, 0)
    route(NB - 1, 0)

    b2_bc, o = at(acc, 0, X, DO)
    b1_bc, o = at(acc, o, X, H)
    qrow = [None, None]
    xt, hid, gel, ysb = [None] * 2, [None] * 2, [None] * 2, [None] * 2
    for p_ in range(2):
        qrow[p_], o = at(acc, o, ROW)
        xt[p_], o = at(acc, o, D)
        hid[p_], o = at(acc, o, H)
        gel[p_], o = at(acc, o, H)
        ysb[p_], o = at(acc, o, DO)
    ge, o = at(acc, o, QT, X)
    gt, o = at(acc, o, QT, X)
    eq_, o = at(acc, o, QT)
    begin, o = at(acc, o, QT)
    live, o = at(acc, o, QT)
    off_i, o = at(acc, o, QT)
    ew_i, o = at(acc, o, QT)
    wcol, o = at(acc, o, QT)
    tokens, o = at(acc, o, QT)
    off_i, ew_i = off_i.bitcast(I32), ew_i.bitcast(I32)
    assert o <= NT * GW and QT <= P
    padrow = sb("padrow", [P, ROW])
    cnt, cnt_i, tls, cum = sb("cnt", [P, X]), sb("cnt_i", [P, X], I32), sb("tls", [P, X]), sb("cum", [P, X])
    pslot_i = sb("pslot_i", [P, X], I32)

    g_xt.wait(sp, B, NB - 1)
    s_b2 = sem("s_b2")
    sp.wait_ge(s_b1, 16)
    sp.dma_start(b1_bc, b1_new.unsqueeze(0).broadcast_to([P, X, H])).then_inc(s_b2, 16)
    sp.dma_start(b2_bc, b2.unsqueeze(0).broadcast_to([P, X, DO])).then_inc(s_b2, 16)

    c3 = Chain(nc, "c3")
    c3.begin()
    c3.then(dve, dve.memset(padrow[:, :], 0.0))
    c3.then(dve, dve.memset(padrow[:, D + 1:D + 2], -1.0))
    c3.then(dve, dve.tensor_scalar(padrow[:, D:D + 1], pcol[:, :], float(N), None, ALU.add))
    c3.then(dve, dve.tensor_scalar(cnt[:, :], carry[:, :], pcol[:, 0:1], None, ALU.add))
    t_pad = c3.then(dve, dve.tensor_copy(pslot_i[:, :], cnt[:, :]))
    c3.wait(pool, t_pad)
    s_pad, s_idle = sem("s_pad"), sem("s_idle")
    for e in range(X):
        pool.indirect_dma_start(queue, bass.IndirectOffsetOnAxis(pslot_i[:, e:e + 1], 0), padrow[:, :], None).then_inc(s_pad, 16)
    c3.wait(sp, t_pad)
    sp.dma_start(queue[IDLE:IDLE + P, :], padrow[:, :]).then_inc(s_idle, 16)
    c3.then(dve, dve.tensor_tensor(cnt[:, :], carry[:, :], qbase[:, :], ALU.subtract))
    c3.then(dve, dve.tensor_scalar(cnt_i[:, :], cnt[:, :], float(P - 1), None, ALU.add))
    c3.then(dve, dve.tensor_scalar(cnt_i[:, :], cnt_i[:, :], P.bit_length() - 1, None, ALU.arith_shift_right))
    c3.then(dve, dve.tensor_copy(tls[:, :], cnt_i[:, :]))
    c3.then(dve, dve.tensor_tensor_scan(cum[:, :], ones[:, 0:X], tls[:, :], 0.0, ALU.mult, ALU.add))
    jcol = iota[:, 0:QT]
    c3.then(dve, dve.tensor_tensor(ge, jcol.unsqueeze(2).broadcast_to([P, QT, X]), cum[:, :].unsqueeze(1).broadcast_to([P, QT, X]), ALU.is_ge))
    c3.then(dve, dve.tensor_tensor(gt, ge, tls[:, :].unsqueeze(1).broadcast_to([P, QT, X]), ALU.mult))
    dve.tensor_reduce(eq_, ge, AX_X, ALU.add)
    c3.then(dve, dve.tensor_reduce(begin, gt, AX_X, ALU.add))
    c3.then(dve, dve.tensor_scalar(live, eq_, float(X), float(P), ALU.is_lt, ALU.mult))
    c3.then(dve, dve.tensor_tensor(begin, jcol, begin, ALU.subtract))
    c3.then(dve, dve.tensor_tensor(begin, begin, live, ALU.mult))
    c3.then(dve, dve.scalar_tensor_tensor(off_i, eq_, float(QUEUE), begin, ALU.mult, ALU.add))
    t_tab = c3.then(dve, dve.tensor_scalar(ew_i, eq_, float(X - 1), None, ALU.min))
    c3.wait(sp, t_tab)
    c3.wait(pe, t_tab)
    c3.wait(dve, t_tab)
    sp.wait_ge(s_pad, 16 * X)
    sp.wait_ge(s_idle, 16)
    for k in range(BUFS):
        sp.wait_ge(s_sc[k], SCATTERS * len(range(k, NB, BUFS)))

    f_tx = Event(nc, "f_tx")
    f_xt = Event(nc, "f_xt")
    f_m1 = Event(nc, "f_m1")
    f_hb = Event(nc, "f_hb")
    f_th = Event(nc, "f_th")
    f_ge = Event(nc, "f_ge")
    f_m2 = Event(nc, "f_m2")
    f_w = Event(nc, "f_w")
    f_ys = Event(nc, "f_ys")
    f_sa = Event(nc, "f_sa", credit_by=pool)
    f_sa.credit = 2
    pool.sem_inc(f_sa.sem, 1)
    s_ld = [sem("s_ld0"), sem("s_ld1")]
    s_add = sem("s_add")
    w_chain = Chain(nc, "w_chain")
    y_chain = Chain(nc, "y_chain")
    tok_idx = sb("tok_idx", [P, 2], I32)
    XT, HID, HT, Y = (0, 1), (2, 3), (4, 5), (6, 7)

    def load_rows(j, par):
        row = sp.value_load(off_i[0:1, ds(j, 1)], min_val=0, max_val=IDLE)
        sp.dma_start(qrow[par], queue[ds(row, P), :]).then_inc(s_ld[par], 16)

    def rows_t(j, par, loads):
        pe.wait_ge(s_ld[par], loads)
        for c in range(DC):
            i = pe.transpose(psum[XT[par]][:, c * P:(c + 1) * P], qrow[par][:, c * P:(c + 1) * P], ident[:, :])
        f_tx.inc(i)
        f_tx.wait(dve, 1, j)
        f_xt.inc(dve.tensor_tensor(xt[par].rearrange("p (c t) -> p c t", c=DC), psum[XT[par]][:, 0:D].rearrange("p (c t) -> p c t", c=DC),
                                   gam[:, :].unsqueeze(2).broadcast_to([P, DC, P]), ALU.mult))

    def weights(j, par, loads):
        dve.wait_ge(s_ld[par], loads)
        dve.tensor_copy(tokens[:, ds(j, 1)], qrow[par][:, D:D + 1])
        w_chain.begin(j)
        w_chain.then(dve, dve.tensor_scalar(wcol[:, ds(j, 1)], qrow[par][:, D + 1:D + 2], eq_[:, ds(j, 1)],
                                            qrow[par][:, D + 2:D + 3], ALU.is_equal, ALU.mult))
        f_w.inc(dve.tensor_scalar(wcol[:, ds(j, 1)], wcol[:, ds(j, 1)], qrow[par][:, D + 3:D + 4], None, ALU.add))

    def layer1(j, par):
        expert = pe.value_load(ew_i[0:1, ds(j, 1)], min_val=0, max_val=X - 1)
        f_xt.wait(pe, 1, j)
        for c in range(DC):
            i = pe.matmul(psum[HID[par]][:, :], xt[par][:, c * P:(c + 1) * P],
                          w1_sb[:, ds(expert, 1), c, :].rearrange("p a h -> p (a h)"), start=(c == 0), stop=(c == DC - 1))
        f_m1.inc(i)

    def bias1(j, par):
        expert = dve.value_load(ew_i[0:1, ds(j, 1)], min_val=0, max_val=X - 1)
        f_m1.wait(dve, 1, j)
        f_hb.inc(dve.tensor_tensor(hid[par], psum[HID[par]][:, :],
                                   b1_bc[:, ds(expert, 1), :].rearrange("p a h -> p (a h)"), ALU.add))

    def next_load(j, par, after):
        f_w.wait(sp, 1, after)
        f_tx.wait(sp, 1, after, apart=True)
        load_rows(j, par)

    load_rows(0, 0)
    load_rows(1, 1)
    g_xt.wait(pe, B, NB - 1)
    g_rk.wait(pe, 1, NB - 1)
    ch.wait(pe, None, NB - 1)
    dve.wait_ge(s_b2, 32)
    for j in range(2):
        rows_t(j, j, 16)
        weights(j, j, 16)
        next_load(j + 2, j, j)
    layer1(0, 0)
    bias1(0, 0)
    pe.wait_ge(s_w2, 16 * X)
    pool.wait_ge(s_out, 16 * (NB + 1))

    with nc.Fori(0, PAIRS) as r:
        for par in range(2):
            j = r * 2 + par
            f_hb.wait(pe, 1, j)
            for k in range(HC):
                i = pe.transpose(psum[HT[par]][:, k * P:(k + 1) * P], hid[par][:, k * P:(k + 1) * P], ident[:, :])
            f_th.inc(i)
            f_th.wait(act, 1, j)
            f_ge.inc(act.activation(gel[par], psum[HT[par]][:, :], ACT.Gelu))
            layer1(j + 1, 1 - par)
            bias1(j + 1, 1 - par)
            rows_t(j + 2, par, r * 16 + 32)
            expert_p = pe.value_load(ew_i[0:1, ds(j, 1)], min_val=0, max_val=X - 1)
            f_ge.wait(pe, 1, j)
            for k in range(HC):
                i = pe.matmul(psum[Y[par]][:, 0:DO], gel[par][:, k * P:(k + 1) * P],
                              w2_sb[:, ds(expert_p, 1), k, :].rearrange("p a o -> p (a o)"), start=(k == 0), stop=(k == HC - 1))
            f_m2.inc(i)
            weights(j + 2, par, r * 16 + 32)
            next_load(j + 4, par, j + 2)
            expert_v = dve.value_load(ew_i[0:1, ds(j, 1)], min_val=0, max_val=X - 1)
            f_sa.wait(dve, 1, j, back=2)
            f_m2.wait(dve, 1, j)
            y_chain.begin(j)
            y_chain.then(dve, dve.tensor_tensor(ysb[par], psum[Y[par]][:, 0:DO],
                                                b2_bc[:, ds(expert_v, 1), :].rearrange("p a o -> p (a o)"), ALU.add))
            dve.tensor_copy(tok_idx[:, par:par + 1], tokens[:, ds(j, 1)])
            f_ys.inc(dve.tensor_scalar(ysb[par], ysb[par], wcol[:, ds(j, 1)], None, ALU.mult))
            f_ys.wait(pool, 1, j, apart=True)
            pool.indirect_dma_start(out, bass.IndirectOffsetOnAxis(tok_idx[:, par:par + 1], 0), ysb[par], None,
                                    compute_op=ALU.add).then_inc(s_add, 16)
            pool.wait_ge(s_add, r * 32 + 16 * (par + 1))
            pool.sem_inc(f_sa.sem, 1)
    sp.wait_ge(s_ld[0], 16 * (PAIRS + 2))
    sp.wait_ge(s_ld[1], 16 * (PAIRS + 2))
    sp.wait_ge(s_add, 16 * 2 * PAIRS)
    sp.wait_ge(s_out, 16 * (NB + 1))


_INS = ['x', 'src', 'dst', 'L0_gnn_W', 'L0_gnn_b', 'L0_ffn_gamma', 'L0_ffn_beta', 'L0_ffn_Wr', 'L0_ffn_br',
        'L0_ffn_W1', 'L0_ffn_b1', 'L0_ffn_W2', 'L0_ffn_b2']


def kernel(**inputs):
    import numpy as _np
    import concourse.bacc as _bacc
    from concourse import mybir as _mybir
    from concourse.bass_utils import run_bass_kernel_spmd as _run

    nc = _bacc.Bacc("TRN2", target_bir_lowering=False, num_devices=1)
    arrays, args = {}, []
    for name in _INS:
        a = _np.ascontiguousarray(inputs[name])
        arrays[f"in_{name}_dram"] = a
        args.append(nc.dram_tensor(f"in_{name}_dram", a.shape, _mybir.dt.from_np(a.dtype), kind="ExternalInput").ap())
    n, d = inputs['x'].shape
    rows = (-(-n // P) + 1) * P
    args.append(nc.dram_tensor("out_dram", (rows, d), _mybir.dt.float32, kind="ExternalOutput").ap())
    build(nc, *args)
    r = _run(nc, [arrays], core_ids=[0])
    return r.results[0]["out_dram"][:n]
```
